# Optimizing a Trainium2 kernel written in Bass

```python
import numpy as np
import jax
import jax.numpy as jnp

def _softmax(x, axis=-1):
    return jax.nn.softmax(x, axis=axis)

def _gelu(x):
    return jax.nn.gelu(x, approximate=True)

def _silu(x):
    return jax.nn.silu(x)

def _sigmoid(x):
    return jax.nn.sigmoid(x)

def _layernorm(x, axis=-1, eps=1e-05):
    m = jnp.mean(x, axis=axis, keepdims=True)
    v = jnp.var(x, axis=axis, keepdims=True)
    return (x - m) / jnp.sqrt(v + eps)

def _scatter_add(tgt, idx, src, axis=0):
    return tgt.at[idx].add(src)

def _segment_sum(src, seg, n):
    return jax.ops.segment_sum(src, seg, n)
kernel_name = 'mk_audio_tower_d1_tok_audfeat2048_r4_d84898'

def setup_inputs(seed: int=0):
    np.random.seed(seed)
    _w = jnp.asarray

    def _rec_inputs():
        import jax
        import jax.numpy as jnp
        _rk = jax.random.key(seed)
        x = -0.000520686 + 1.00062 * jax.random.normal(jax.random.fold_in(_rk, 1), (64, 750, 1), jnp.float32)
        return x
    x = _rec_inputs()

    def _L0_tok_setup():
        import jax, jax.numpy as jnp
        import numpy as np
        PATCH_LEN = 128
        D_MODEL = 512
        BATCH = 128
        SEQ_LEN = 4096
        FEATURES = 1
        key = jax.random.key(seed)
        k1, k2, k3 = jax.random.split(key, 3)
        x = jax.random.normal(k1, (BATCH, SEQ_LEN, FEATURES), dtype=jnp.float32)
        W = jax.random.normal(k2, (D_MODEL, PATCH_LEN), dtype=jnp.float32) * (1.0 / np.sqrt(PATCH_LEN))
        b = jax.random.normal(k3, (D_MODEL,), dtype=jnp.float32) * 0.01
        return {'x': x, 'W': W, 'b': b}
    _L0_tok_all = _L0_tok_setup()
    _L0_tok_in = {k: v for k, v in _L0_tok_all.items() if k in ('W', 'b')}
    del _L0_tok_all

    def _L0_attn_setup():
        import jax, jax.numpy as jnp
        import numpy as np
        import math
        B, SEQ, DIM, HEADS = (1, 512, 512, 8)
        L_INIT = 0.8 - 0.6 * math.exp(-0.3 * 1)
        EPS = 1e-06
        key = jax.random.key(seed)
        ks = jax.random.split(key, 9)
        x = jax.random.normal(ks[0], (B, SEQ, DIM), jnp.float32)
        l_q1 = jax.random.normal(ks[1], (HEADS,), jnp.float32) * 0.1
        l_k1 = jax.random.normal(ks[2], (HEADS,), jnp.float32) * 0.1
        l_q2 = jax.random.normal(ks[3], (HEADS,), jnp.float32) * 0.1
        l_k2 = jax.random.normal(ks[4], (HEADS,), jnp.float32) * 0.1
        s = 1.0 / math.sqrt(DIM)
        wq = jax.random.normal(ks[5], (2 * DIM, DIM), jnp.float32) * s
        wk = jax.random.normal(ks[6], (2 * DIM, DIM), jnp.float32) * s
        wv = jax.random.normal(ks[7], (DIM, DIM), jnp.float32) * s
        wo = jax.random.normal(ks[8], (DIM, DIM), jnp.float32) * s
        return {'x': x, 'l_q1': l_q1, 'l_k1': l_k1, 'l_q2': l_q2, 'l_k2': l_k2, 'wq': wq, 'wk': wk, 'wv': wv, 'wo': wo}
    _L0_attn_all = _L0_attn_setup()
    _L0_attn_in = {k: v for k, v in _L0_attn_all.items() if k in ('l_q1', 'l_k1', 'l_q2', 'l_k2', 'wq', 'wk', 'wv', 'wo')}
    del _L0_attn_all

    def _L0_ffn_setup():
        import jax, jax.numpy as jnp
        import numpy as np
        B, S, D, H = (8, 1024, 512, 1280)

        def ternarize_weight(w):
            abs_mean = jnp.maximum(jnp.mean(jnp.abs(w)), 1e-05)
            thr = 0.7 * abs_mean
            one = jnp.ones((), dtype=w.dtype)
            q = jnp.where(w > thr, one, jnp.where(w < -thr, -one, jnp.zeros((), dtype=w.dtype)))
            return w + jax.lax.stop_gradient(q * abs_mean - w)
        key = jax.random.key(seed)
        k1, k2, k3 = jax.random.split(key, 3)
        x = jax.random.normal(k1, (B, S, D), dtype=jnp.float32)
        w_fc = jax.random.normal(k2, (H, D), dtype=jnp.float32) / np.sqrt(D).astype(np.float32)
        w_proj = jax.random.normal(k3, (D, H), dtype=jnp.float32) / np.sqrt(H).astype(np.float32)
        return {'x': x, 'w_fc': w_fc, 'w_proj': w_proj}
    _L0_ffn_all = _L0_ffn_setup()
    _L0_ffn_in = {k: v for k, v in _L0_ffn_all.items() if k in ('w_fc', 'w_proj')}
    del _L0_ffn_all
    return {'x': x, 'L0_tok_W': _L0_tok_in['W'], 'L0_tok_b': _L0_tok_in['b'], 'L0_attn_l_q1': _L0_attn_in['l_q1'], 'L0_attn_l_k1': _L0_attn_in['l_k1'], 'L0_attn_l_q2': _L0_attn_in['l_q2'], 'L0_attn_l_k2': _L0_attn_in['l_k2'], 'L0_attn_wq': _L0_attn_in['wq'], 'L0_attn_wk': _L0_attn_in['wk'], 'L0_attn_wv': _L0_attn_in['wv'], 'L0_attn_wo': _L0_attn_in['wo'], 'L0_ffn_w_fc': _L0_ffn_in['w_fc'], 'L0_ffn_w_proj': _L0_ffn_in['w_proj']}

def reference(x, L0_tok_W, L0_tok_b, L0_attn_l_q1, L0_attn_l_k1, L0_attn_l_q2, L0_attn_l_k2, L0_attn_wq, L0_attn_wk, L0_attn_wv, L0_attn_wo, L0_ffn_w_fc, L0_ffn_w_proj):
    import jax
    import jax.numpy as jnp

    def _L0_tok_ref(x, W, b):
        import jax, jax.numpy as jnp
        import numpy as np
        PATCH_LEN = 128
        D_MODEL = 512
        BATCH = 128
        SEQ_LEN = 4096
        FEATURES = 1
        B, S, F = x.shape
        P = PATCH_LEN
        stride = P // 2
        starts = jnp.arange(0, S - P + 1, stride)
        idx = starts[:, None] + jnp.arange(P)
        patches = x[:, idx, :].reshape(B, starts.shape[0], P * F)
        patches = patches[:, :, :P]
        return jnp.einsum('bnp,dp->bnd', patches, W) + b

    def _L0_attn_ref(x, l_q1, l_k1, l_q2, l_k2, wq, wk, wv, wo):
        import jax, jax.numpy as jnp
        import numpy as np
        import math
        B, SEQ, DIM, HEADS = (1, 512, 512, 8)
        L_INIT = 0.8 - 0.6 * math.exp(-0.3 * 1)
        EPS = 1e-06
        b, s, d = x.shape
        nh = HEADS
        lmbda = jnp.exp(jnp.sum(l_q1 * l_k1)) - jnp.exp(jnp.sum(l_q2 * l_k2)) + L_INIT
        q = jnp.einsum('bsd,od->bso', x, wq)
        k = jnp.einsum('bsd,od->bso', x, wk)
        v = jnp.einsum('bsd,od->bso', x, wv)

        def split_heads(t):
            return t.reshape(b, s, nh, -1).transpose(0, 2, 1, 3)
        q, k, v = map(split_heads, (q, k, v))

        def prep(t):
            dh = t.shape[-1] // 2
            t = t.reshape(b, nh, s, 2, dh)
            return t.transpose(0, 1, 3, 2, 4).reshape(b, nh * 2, s, dh)
        q, k = (prep(q), prep(k))
        dh = q.shape[-1]
        scores = jnp.einsum('bhqd,bhkd->bhqk', q, k) / math.sqrt(dh)
        causal = jnp.triu(jnp.full((s, s), -jnp.inf, dtype=scores.dtype), 1)
        attn = jax.nn.softmax((scores + causal[None, None]).astype(jnp.float32), axis=-1).astype(scores.dtype)
        attn = attn[:, :nh] - attn[:, nh:] * lmbda
        out = jnp.einsum('bhqk,bhkd->bhqd', attn, v)
        dv = out.shape[-1]
        o = out.reshape(b, nh, s, nh, dv // nh)
        o32 = o.astype(jnp.float32)
        o = (o32 * jax.lax.rsqrt(jnp.mean(o32 * o32, axis=-1, keepdims=True) + EPS)).astype(o.dtype)
        o = o.reshape(b, nh, s, dv) * (1.0 - L_INIT)
        o = o.transpose(0, 2, 1, 3).reshape(b, s, nh * dv)
        return jnp.einsum('bsd,od->bso', o, wo)

    def _L0_ffn_ref(x, w_fc, w_proj):
        import jax, jax.numpy as jnp
        import numpy as np
        B, S, D, H = (8, 1024, 512, 1280)

        def ternarize_weight(w):
            abs_mean = jnp.maximum(jnp.mean(jnp.abs(w)), 1e-05)
            thr = 0.7 * abs_mean
            one = jnp.ones((), dtype=w.dtype)
            q = jnp.where(w > thr, one, jnp.where(w < -thr, -one, jnp.zeros((), dtype=w.dtype)))
            return w + jax.lax.stop_gradient(q * abs_mean - w)
        h = jnp.einsum('bsd,hd->bsh', x, ternarize_weight(w_fc))
        h = jnp.square(jax.nn.relu(h))
        return jnp.einsum('bsh,dh->bsd', h, ternarize_weight(w_proj))
    h = _L0_tok_ref(x, L0_tok_W, L0_tok_b)
    h = h + _L0_attn_ref(_layernorm(h, axis=-1), L0_attn_l_q1, L0_attn_l_k1, L0_attn_l_q2, L0_attn_l_k2, L0_attn_wq, L0_attn_wk, L0_attn_wv, L0_attn_wo)
    h = h + _L0_ffn_ref(_layernorm(h, axis=-1), L0_ffn_w_fc, L0_ffn_w_proj)
    return h

_drawn_inputs = setup_inputs


def setup_inputs(seed=0):
    import zlib

    import numpy as np

    out = dict(_drawn_inputs(seed))
    spreads = {}
    factors = {'L0_tok_b': 4.252, 'L0_attn_l_q1': 2.733, 'L0_attn_l_k2': 8.0}
    for name, (base, spread) in spreads.items():
        noise = np.random.default_rng([zlib.crc32(name.encode()), seed]).standard_normal(out[name].shape)
        drawn = base * np.exp(spread * noise) if base else spread * noise
        out[name] = jnp.asarray(drawn.astype(out[name].dtype))
    for name, factor in factors.items():
        out[name] = (out[name] * factor).astype(out[name].dtype)
    return out
```

```python
import math
from contextlib import ExitStack

import concourse.bass as bass
from concourse import mybir

F32 = mybir.dt.float32
F32R = mybir.dt.float32r
F16 = mybir.dt.float16
BF16 = mybir.dt.bfloat16
I32 = mybir.dt.int32
ALU = mybir.AluOpType
ACT = mybir.ActivationFunctionType
AX = mybir.AxisListType

P = 128
NB, NPATCH, STRIDE = 64, 10, 64
D, NH, DH = 512, 8, 64
HID = 1280
KD = D // P
HC = HID // P
TOK = NB * NPATCH
TT = TOK // P
GTOK = 6 * NPATCH
GP = 64
NG = -(-TOK // GTOK)
NT = -(-NG // 2)
TOKG = NG * GTOK
NPAIR = 2 * NH // 2
NHP = NH // 2
QKV = 5 * D
PIECE = 256
NPC = QKV // PIECE
FW = P + 1
FWS = 132
L_INIT = 0.8 - 0.6 * math.exp(-0.3 * 1)
LN_EPS, RMS_EPS = 1e-5, 1e-6
RMSW = 8
MASKED = -1.0e30
Z_SCALE = 2.0 ** 11
H_SCALE = 2.0 ** -2
HALF_G = (6, NG - 6)
FFN_TILES = ((0, 2), (2, TT))
QK_ORDER = [c for j in range(NPAIR) for c in (j, NPAIR + j)]


def audio_block(nc, xT, w_pos, w_col, b, lam, wqkv, wo, w_fc, w_proj, out):
    with ExitStack() as ctx:
        def at(name, shape, dtype, offset):
            return nc.alloc_sbuf_tensor_at(name, shape, dtype, offset=offset)

        def sem(name):
            return ctx.enter_context(nc.semaphore(name))

        top = [(nc.sbuf_base + 31) // 32 * 32]

        def region(size):
            start = top[0]
            top[0] += (size + 31) // 32 * 32
            return start

        ones = at("ones", [P, P], F32, region(512))
        mean_w = at("mean_w", [P, P], F32, region(512))
        ident = at("ident", [P, P], F32, region(512))
        ident_b = at("ident_b", [P, P], BF16, region(256))
        mask = at("mask", [P, NPAIR, GP], BF16, region(1024))
        cv_b = at("cv_b", [P, D], F32, region(2048))
        r_b = at("r_b", [P, TOKG], F32, region(4 * TOKG))
        ph = at("ph", [P, 2 * NT, GP], F32R, region(3072))
        pl = at("pl", [P, 2 * NT, GP], F32R, region(3072))
        h = at("h", [P, TT, D], F32, region(4 * TT * D))
        sel = at("sel", [P, GTOK], F32, region(4 * GTOK))
        cbias = at("cbias", [P, QKV // P], F32, region(4 * 20))
        lamt = at("lamt", [P, 2, 2, NH], F32, region(128))
        lamp = at("lamp", [P, 2, NH], F32, region(64))
        lams = at("lams", [P, 2], F32, region(8))
        lame = at("lame", [P, 2], F32, region(8))
        neglam = at("neglam", [P, 1], F32, region(4))
        bnst = at("bnst", [P, TT, 6], F32, region(120))
        stat = at("stat", [P, TT, 2], F32, region(40))
        stat2 = at("stat2", [P, TT, 2], F32, region(40))
        rtok = at("rtok", [P, TT], F32, region(20))
        rtok2 = at("rtok2", [P, TT], F32, region(20))
        rq = at("rq", [P, 2 * NT], F32, region(48))
        rq8 = at("rq8", [P, 2 * NT], F32, region(48))
        rk = at("rk", [P, NT], F32, region(24))
        nx = at("nx", [P, 64], F32, region(256))
        nt_ = at("nt_", [P, 64], F32, region(256))
        ny = at("ny", [P, 64], I32, region(256))
        mx = at("mx", [P, 2, NPAIR], F32, region(64))
        ssum = at("ssum", [P, 2, NPAIR], F32, region(64))
        sinv = at("sinv", [P, 4, NPAIR], F32, region(128))
        ratio = at("ratio", [P, 3, NHP], F32, region(48))
        ms = at("ms", [P, 64], F32, region(256))
        part = at("part", [P, HC], F32, region(40))
        psm = at("psm", [P, 2], F32, region(8))
        am = at("am", [P, 2], F32, region(8))
        thr = at("thr", [P, 2, 2], F32, region(16))
        sout = at("sout", [P, 1], F32, region(4))

        ra = region(4 * KD * QKV)
        wqkv_s = at("wqkv_s", [P, NPC, KD, PIECE], F32, ra)
        fc_raw = at("fc_raw", [P, KD, HID], F32, ra)
        proj_raw = at("proj_raw", [P, HC, D], F32, ra + 4 * KD * HID)
        qproj = at("qproj", [P, HC, D], F16, ra)
        z = [at(f"z{i}", [P, D], F32, ra + 10240 + 2048 * i) for i in range(2)]
        orow = [at(f"orow{i}", [P, D], F32, ra + 14336 + 2048 * i) for i in range(2)]

        rqd = region(4 * NPAIR * NG * 2 * GP)
        qbd = at("qbd", [P, NPAIR, NG, 2, GP], F32, rqd)
        zth = at("zth", [P, KD, TOK], F16, rqd)
        ztl = at("ztl", [P, KD, TOK], F16, rqd + 5120)
        gh = at("gh", [P, HC, TOK], F16, rqd + 10240)
        gl = at("gl", [P, HC, TOK], F16, rqd + 23040)
        rel = [at(f"rel{i}", [P, 384], F32, rqd + 35840 + 1536 * i) for i in range(2)]
        squ = [at(f"squ{i}", [P, 384], F32, rqd + 38912 + 1536 * i) for i in range(2)]

        rkt = region(4 * NPAIR * TOKG)
        kt = at("kt", [P, NPAIR, TOKG], F32, rkt)
        woh = at("woh", [P, KD, D], F32R, rkt)
        wol = at("wol", [P, KD, D], F32R, rkt + 8192)

        v = at("v", [P, NT, D], F32, region(4 * NT * D))

        rm = region(4 * (QKV // P) * FW)
        mt = at("mt", [P, QKV // P, FW], F32, rm)
        wo_raw = at("wo_raw", [P, KD, D], F32, rm)

        rmm = region(8 * NHP * TOKG)
        mh = at("mh", [P, QKV], F32R, rmm)
        ml = at("ml", [P, QKV], F32R, rmm + 4 * QKV)
        oth = at("oth", [P, NHP, TOKG], F32R, rmm)
        otl = at("otl", [P, NHP, TOKG], F32R, rmm + 4 * NHP * TOKG)

        qfc = at("qfc", [P, KD, HID], F16, region(2 * KD * HID))

        rw = region(20480)
        pt = at("pt", [P, TOK], F32, rw)
        wcol = at("wcol", [P, D], F32, rw + 2560)
        wpos = at("wpos", [P, KD, FW], F32, rw + 4608)
        wc = at("wc", [P, KD, FW], F32, rw + 6688)
        b_b = at("b_b", [P, D], F32, rw + 8768)
        diag = at("diag", [P, TT, P], F32, rw + 10816)
        rsel = at("rsel", [P, NG, GTOK], F32, rw + 10816 + 2560)
        e = [at(f"e{i}", [P, NPAIR, GP], F32, rw + 2048 * i) for i in range(3)]
        a = [at(f"a{i}", [P, NHP, 2, GP], F32, rw + 6144 + 2048 * i) for i in range(2)]
        ats = [at(f"ats{i}", [P, NHP, 2, GP], F32, rw + 10240 + 2048 * i) for i in range(2)]
        on = [at(f"on{i}", [P, 2, NHP, DH], F32, rw + 14336 + 2048 * i) for i in range(2)]
        osq = at("osq", [P, 2, NHP, DH], F32, rw + 18432)
        assert top[0] <= nc.sbuf_usable_end, (top[0], nc.sbuf_usable_end)

        bank = [ctx.enter_context(nc.psum_tensor(f"bank{i}", [P, 512], F32)) for i in range(3)]
        o_ps = ctx.enter_context(nc.psum_tensor("o_ps", [P, 2, 512], F32))
        bank += [o_ps[:, 0, :], o_ps[:, 1, :]]
        bank += [ctx.enter_context(nc.psum_tensor(f"bank{i}", [P, 512], F32)) for i in range(5, 8)]
        bank = [x[:, :] for x in bank]
        h_acc = (bank[0], bank[5])
        fold_acc = (bank[1], bank[2])
        m_acc = (bank[3], bank[4])
        rb_acc = (bank[6], bank[7])
        cv_acc = bank[0]
        mean_acc = bank[6]
        ring = bank[5:8]
        s_acc = bank[0:2]
        at_acc = bank[2]
        wo_acc = bank[5:7]
        zt_acc = (bank[7], bank[2])
        fc_acc = bank[0:2]
        pj_acc = (bank[3], bank[4])

        ld_x, ld_w, ld_lam, ld_b, ld_wo = sem("ld_x"), sem("ld_w"), sem("ld_lam"), sem("ld_b"), sem("ld_wo")
        ld_qkv = [sem(f"ld_qkv{f}") for f in range(NPC)]
        ld_fc, ld_proj = sem("ld_fc"), sem("ld_proj")
        st_out = [sem(f"st_out{i}") for i in range(2)]
        consts = sem("consts")
        pchain = sem("pchain")
        zeros = sem("zeros")
        ph_rdy, pl_rdy = sem("ph_rdy"), sem("pl_rdy")
        mean_rdy, wc_rdy = sem("mean_rdy"), sem("wc_rdy")
        h_mm, h_ev = sem("h_mm"), sem("h_ev")
        fold_mm, mt_rdy = sem("fold_mm"), sem("mt_rdy")
        tr_mm, mh_rdy, ml_rdy = sem("tr_mm"), sem("mh_rdy"), sem("ml_rdy")
        dg_rdy, rb_mm, rb_rdy, rk_rdy = sem("dg_rdy"), sem("rb_mm"), sem("rb_rdy"), sem("rk_rdy")
        cb_rdy, dv_rdy, cv_mm, cv_rdy = sem("cb_rdy"), sem("dv_rdy"), sem("cv_mm"), sem("cv_rdy")
        ring_mm = sem("ring_mm")
        q_ev = sem("q_ev")
        kv_ev = sem("kv_ev")
        s_mm, d_rdy, e_rdy, rat_rdy, a_rdy = sem("s_mm"), sem("d_rdy"), sem("e_rdy"), sem("rat_rdy"), sem("a_rdy")
        at_mm, at_rdy, av_mm, on_rdy, sq_rdy = sem("at_mm"), sem("at_rdy"), sem("av_mm"), sem("on_rdy"), sem("sq_rdy")
        rms_rdy, on2_rdy, ot_mm, oth_rdy, otl_rdy = (sem("rms_rdy"), sem("on2_rdy"), sem("ot_mm"), sem("oth_rdy"),
                                                     sem("otl_rdy"))
        lsum_rdy, lexp_rdy = sem("lsum_rdy"), sem("lexp_rdy")
        ab_rdy, ab_mm = sem("ab_rdy"), sem("ab_mm")
        qfc_rdy, qproj_rdy, wos_rdy = sem("qfc_rdy"), sem("qproj_rdy"), sem("wos_rdy")
        wo_mm, h1_rdy, z_rdy, zt_mm, zth_rdy, ztl_rdy = (sem("wo_mm"), sem("h1_rdy"), sem("z_rdy"), sem("zt_mm"),
                                                         sem("zth_rdy"), sem("ztl_rdy"))
        fc_mm, rel_rdy, squ_rdy, gh_rdy, gl_rdy = (sem("fc_mm"), sem("rel_rdy"), sem("squ_rdy"), sem("gh_rdy"),
                                                   sem("gl_rdy"))
        pj_mm, o_rdy = sem("pj_mm"), sem("o_rdy")
        vchain = sem("vchain")

        uses = [("qk", 0, c) for c in QK_ORDER] + [("v", T, 0) for T in range(3)]
        n_first = len(uses)
        uses += [("qk", 1, c) for c in QK_ORDER] + [("v", T, 0) for T in range(3, NT)]
        n_uses = len(uses)
        cut = [n_first + (n_uses - n_first) * i // 4 for i in range(5)]

        def is_q(u):
            return uses[u][0] == "qk" and uses[u][2] < NPAIR

        def evacuated(u):
            n = sum(is_q(w) for w in range(u + 1))
            return (q_ev, n) if is_q(u) else (kv_ev, u + 1 - n)

        def groups(half):
            return (0, HALF_G[0]) if half == 0 else (HALF_G[0], NG)

        def gps(T):
            return range(min(2, NG - 2 * T))

        n_kv = n_uses - NPAIR * 2

        block = ctx.enter_context(nc.Block())

        @block.sync
        def _(sp):
            sp.dma_start(pt[:, :], xT).then_inc(ld_x, 16)
            sp.dma_start(wpos[:, :, :], w_pos).then_inc(ld_w, 16)
            sp.dma_start(wcol[:, :], w_col).then_inc(ld_w, 16)
            sp.dma_start(b_b[:, :], b.partition_broadcast(P)).then_inc(ld_b, 16)
            sp.dma_start(lamt[:, :, :, :], lam.partition_broadcast(P)).then_inc(ld_lam, 16)
            for f in range(NPC):
                sp.dma_start(wqkv_s[:, f, :, :], wqkv[f]).then_inc(ld_qkv[f], 16)
            sp.wait_ge(fold_mm, NPC // 2)
            sp.dma_start(fc_raw[:, :, :], w_fc).then_inc(ld_fc, 16)
            sp.wait_ge(fold_mm, NPC)
            sp.dma_start(proj_raw[:, :, :], w_proj).then_inc(ld_proj, 16)
            sp.wait_ge(tr_mm, NPC)
            sp.wait_ge(cb_rdy, 1)
            sp.dma_start(wo_raw[:, :, :], wo).then_inc(ld_wo, 16)
            for i in range(TT):
                sp.wait_ge(o_rdy, i + 1)
                sp.dma_start(out[i], orow[i % 2][:, :]).then_inc(st_out[i % 2], 16)
            for i in range(2):
                sp.wait_ge(st_out[i], 16 * len(range(i, TT, 2)))

        @block.gpsimd
        def _(pool):
            n = [0]

            def link(ins):
                n[0] += 1
                ins.then_inc(pchain, 1)
                pool.wait_ge(pchain, n[0])

            pool.memset(mean_w[:, :], 1.0 / D).then_inc(consts, 1)
            pool.memset(ones[:, :], 1.0).then_inc(consts, 1)
            link(pool.memset(ident[:, :], 0.0))
            pool.affine_select(out=ident[:, :], in_=ident[:, :], compare_op=ALU.not_equal, fill=1.0, base=0,
                               pattern=[[-1, P]], channel_multiplier=1).then_inc(consts, 1)
            for t in (ph, pl):
                pool.memset(t[:, :, GTOK:].bitcast(F32), 0.0)
                pool.memset(t[:, NG - 1, TOK - (NG - 1) * GTOK:GTOK].bitcast(F32), 0.0)
                pool.memset(t[:, NG, 0:GTOK].bitcast(F32), 0.0)
            pool.memset(rq[:, NG:], 0.0)
            pool.memset(r_b[:, TOK:], 0.0).then_inc(zeros, 1)
            pool.wait_ge(consts, 3)
            pool.wait_ge(zeros, 1)
            pool.tensor_copy(ident_b[:, :], ident[:, :]).then_inc(consts, 1)
            for half in range(2):
                s = GP * half
                pool.wait_ge(consts, 4 + half)
                pool.tensor_copy(sel[s:s + GP, :], ident[s:s + GP, s:s + GTOK]).then_inc(consts, 1)
            pool.wait_ge(consts, 6)
            link(pool.memset(mask[:, :, 0:GTOK], 0.0))
            link(pool.memset(mask[:, :, GTOK:], MASKED))
            for half in range(2):
                s = GP * half
                m = mask[s:s + GP, :, 0:GTOK]
                link(pool.affine_select(out=m, in_=m, compare_op=ALU.is_ge, fill=MASKED, base=NPATCH - 1,
                                        pattern=[[0, NPAIR], [NPATCH, 6], [0, NPATCH]], channel_multiplier=-1))
                last = pool.affine_select(out=m, in_=m, compare_op=ALU.is_ge, fill=MASKED, base=0,
                                          pattern=[[0, NPAIR], [-1, GTOK]], channel_multiplier=1)
                if half == 0:
                    link(last)
            last.then_inc(consts, 1)
            pool.wait_ge(consts, 7)
            blocks = qbd[:, :, :, :, :].rearrange("p c g a q -> p (c g) (a q)")
            link(pool.memset(blocks[0:GP, :, GTOK:], 0.0))
            link(pool.memset(blocks[GP:P, :, 0:GP], 0.0))
            pool.memset(blocks[GP:P, :, GP + GTOK:], 0.0).then_inc(zeros, 1)
            pool.wait_ge(zeros, 2)
            pool.wait_ge(mt_rdy, NPC)
            pool.tensor_copy(cbias[:, :], mt[:, :, P]).then_inc(cb_rdy, 1)

            for T in range(NT + 1):
                if T < NT:
                    for i in gps(T):
                        g = 2 * T + i
                        eg, ag = e[g % 3], a[T % 2]
                        if T >= 2 and i == 0:
                            pool.wait_ge(at_mm, T - 1)
                        pool.wait_ge(rat_rdy, g + 1)
                        link(pool.tensor_tensor(eg[:, NHP:, :], eg[:, NHP:, :],
                                                ratio[:, g % 3, :].unsqueeze(2).to_broadcast([P, NHP, GP]), ALU.mult))
                        pool.tensor_tensor(ag[:, :, i, :], eg[:, NHP:, :], eg[:, 0:NHP, :], ALU.add).then_inc(a_rdy, 1)
                if T >= 1:
                    n_gp = len(gps(T - 1))
                    w = on[(T - 1) % 2][:, 0:n_gp].rearrange("p g j (c d) -> p (g j c) d", d=RMSW)
                    pool.wait_ge(rms_rdy, T)
                    y = ny[:, 0:32 * n_gp].bitcast(F32)
                    pool.tensor_tensor(w, w, y.unsqueeze(2).to_broadcast([P, 32 * n_gp, RMSW]),
                                       ALU.mult).then_inc(on2_rdy, 1)
                if T == NT - 1:
                    pool.wait_ge(ld_wo, 16)
                    pool.wait_ge(s_mm, NG)
                    link(pool.tensor_copy(woh[:, :, :], wo_raw[:, :, :]))
                    pool.tensor_tensor(wol[:, :, :], wo_raw[:, :, :], woh[:, :, :].bitcast(F32),
                                       ALU.subtract).then_inc(wos_rdy, 1)
            for k in range(2 * HC):
                n_tok = P * (FFN_TILES[k // HC][1] - FFN_TILES[k // HC][0])
                pool.wait_ge(rel_rdy, k + 1)
                if k >= 2:
                    pool.wait_ge(gl_rdy, k - 1)
                r_ = rel[k % 2][:, 0:n_tok]
                pool.tensor_tensor(squ[k % 2][:, 0:n_tok], r_, r_, ALU.mult).then_inc(squ_rdy, 1)

        @block.scalar
        def _(act):
            full = (NG - 1)
            rest = TOK - full * GTOK
            act.wait_ge(ld_x, 16)
            act.activation(ph[:, 0:full, 0:GTOK], pt[:, 0:full * GTOK].rearrange("p (g q) -> p g q", q=GTOK), ACT.Copy)
            act.activation(ph[:, full, 0:rest], pt[:, full * GTOK:], ACT.Copy).then_inc(ph_rdy, 1)

            def m_hi(f):
                act.wait_ge(tr_mm, f + 1)
                act.activation(mh[:, f * PIECE:(f + 1) * PIECE], m_acc[f % 2][:, 0:PIECE], ACT.Copy).then_inc(mh_rdy, 1)

            for f in range(NPC):
                act.wait_ge(fold_mm, f + 1)
                act.activation(mt[:, 2 * f:2 * f + 2, :],
                               fold_acc[f % 2][:, 0:2 * FWS].rearrange("p (c w) -> p c w", w=FWS)[:, :, 0:FW],
                               ACT.Copy).then_inc(mt_rdy, 1)
                if f >= 1:
                    m_hi(f - 1)
                if f == 3:
                    act.wait_ge(rb_mm, 1)
                    for i in range(2):
                        last = act.activation(r_b[:, 320 * i:320 * i + 320], rb_acc[i][:, 0:320], ACT.Copy)
                    last.then_inc(rb_rdy, 1)
            m_hi(NPC - 1)
            act.wait_ge(lsum_rdy, 1)
            act.activation(lame[:, :], lams[:, :], ACT.Exp).then_inc(lexp_rdy, 1)

            def evacuate(u0, u1):
                for u in range(u0, u1):
                    if is_q(u):
                        _, half, c = uses[u]
                        g0, g1 = groups(half)
                        act.wait_ge(ring_mm, u + 1)
                        for s in range(2):
                            r0 = GP * s
                            last = act.activation(
                                qbd[r0:r0 + GP, c, g0:g1, s, 0:GTOK],
                                ring[u % 3][r0:r0 + GP, 0:(g1 - g0) * GTOK].rearrange("p (g q) -> p g q", q=GTOK),
                                ACT.Identity, bias=cbias[r0:r0 + GP, c:c + 1])
                        last.then_inc(q_ev, 1)

            act.wait_ge(zeros, 2)
            act.wait_ge(cb_rdy, 1)
            evacuate(0, n_first)
            for T in range(NT + 2):
                if T < NT:
                    for i in gps(T):
                        g = 2 * T + i
                        act.wait_ge(d_rdy, g + 1)
                        act.activation(e[g % 3][:, :, :], e[g % 3][:, :, :], ACT.Exp,
                                       scale=rq8[:, g:g + 1]).then_inc(e_rdy, 1)
                if T < 2:
                    evacuate(cut[2 * T], cut[2 * T + 1])
                if 1 <= T <= NT:
                    act.wait_ge(at_mm, T)
                    if T >= 3:
                        act.wait_ge(av_mm, T - 2)
                    act.activation(ats[(T - 1) % 2][:, :, :, :], at_acc.rearrange("p (j h q) -> p j h q", h=2, q=GP),
                                   ACT.Copy, scale=rk[:, T - 1:T]).then_inc(at_rdy, 1)
                if T < 2:
                    evacuate(cut[2 * T + 1], cut[2 * T + 2])
                if T >= 2:
                    act.wait_ge(ot_mm, T - 1)
                    for i in gps(T - 2):
                        g = 2 * (T - 2) + i
                        for j in range(2):
                            last = act.activation(
                                oth[:, 2 * j:2 * j + 2, g * GTOK:(g + 1) * GTOK],
                                at_acc[:, (2 * i + j) * P:(2 * i + j + 1) * P].rearrange(
                                    "p (h q) -> p h q", q=GP)[:, :, 0:GTOK], ACT.Copy)
                    last.then_inc(oth_rdy, 1)
                if 1 <= T <= NT:
                    act.wait_ge(on_rdy, T)
                    n_gp = len(gps(T - 1))
                    act.activation(osq[:, 0:n_gp, :, :], on[(T - 1) % 2][:, 0:n_gp, :, :], ACT.Square).then_inc(sq_rdy, 1)

            def z_hi(i):
                act.wait_ge(zt_mm, i + 1)
                act.activation(zth[:, :, i * P:(i + 1) * P], zt_acc[i % 2].rearrange("p (k t) -> p k t", t=P),
                               ACT.Copy).then_inc(zth_rdy, 1)

            def g_hi(k):
                half, c = divmod(k, HC)
                t0, t1 = FFN_TILES[half]
                act.wait_ge(squ_rdy, k + 1)
                act.activation(gh[:, c, t0 * P:t1 * P], squ[k % 2][:, 0:(t1 - t0) * P], ACT.Copy).then_inc(gh_rdy, 1)

            for i in range(TT):
                z_hi(i)
            for k in range(2 * HC):
                half, c = divmod(k, HC)
                n_tok = (FFN_TILES[half][1] - FFN_TILES[half][0]) * P
                act.wait_ge(fc_mm, k + 1)
                if k >= 2:
                    act.wait_ge(squ_rdy, k - 1)
                act.activation(rel[k % 2][:, 0:n_tok], fc_acc[k % 2][:, 0:n_tok], ACT.Relu,
                               scale=H_SCALE / Z_SCALE).then_inc(rel_rdy, 1)
                if k >= 1:
                    g_hi(k - 1)
            g_hi(2 * HC - 1)

        @block.vector
        def _(dve):
            n = [0]

            def link(ins):
                n[0] += 1
                ins.then_inc(vchain, 1)
                dve.wait_ge(vchain, n[0])

            def rsqrt(y, x, t):
                yf = y.bitcast(F32)
                link(dve.tensor_scalar(y, x.bitcast(I32), 1, None, ALU.logical_shift_right))
                link(dve.tensor_scalar(y, y, -1.0, float(0x5F3759DF), ALU.mult, ALU.add))
                for step in range(3):
                    link(dve.scalar_tensor_tensor(t, yf, -0.5, yf, ALU.mult, ALU.mult))
                    link(dve.tensor_tensor(t, t, x, ALU.mult))
                    last = dve.scalar_tensor_tensor(yf, t, 1.5, yf, ALU.add, ALU.mult)
                    if step < 2:
                        link(last)
                return last

            dve.wait_ge(mean_rdy, 1)
            dve.tensor_tensor(wc[:, :, :], wpos[:, :, :], mean_acc[:, 0:FW].unsqueeze(1).to_broadcast([P, KD, FW]),
                              ALU.subtract).then_inc(wc_rdy, 1)
            dve.wait_ge(ld_b, 16)
            for i in range(TT):
                dve.wait_ge(h_mm, i + 1)
                dve.tensor_tensor(h[:, i, :], h_acc[i % 2], b_b[:, :], ALU.add).then_inc(h_ev, 1)
                dve.wait_ge(h_ev, i + 1)
                link(dve.bn_stats(bnst[:, i, :], h[:, i, :]))
                link(dve.bn_aggr(stat[:, i, :], bnst[:, i, :]))
            link(dve.tensor_scalar(nx[:, 0:TT], stat[:, :, 1], LN_EPS, None, ALU.add))
            link(rsqrt(ny[:, 0:TT], nx[:, 0:TT], nt_[:, 0:TT]))
            dve.wait_ge(consts, 3)
            dve.tensor_tensor(diag[:, :, :], ident[:, :].unsqueeze(1).to_broadcast([P, TT, P]),
                              ny[:, 0:TT].bitcast(F32).unsqueeze(2).to_broadcast([P, TT, P]),
                              ALU.mult).then_inc(dg_rdy, 1)
            full = NG - 1
            rest = TOK - full * GTOK
            dve.wait_ge(ph_rdy, 1)
            dve.tensor_tensor(pl[:, 0:full, 0:GTOK], pt[:, 0:full * GTOK].rearrange("p (g q) -> p g q", q=GTOK),
                              ph[:, 0:full, 0:GTOK].bitcast(F32), ALU.subtract)
            dve.tensor_tensor(pl[:, full, 0:rest], pt[:, full * GTOK:], ph[:, full, 0:rest].bitcast(F32),
                              ALU.subtract).then_inc(pl_rdy, 1)
            dve.wait_ge(ld_lam, 16)
            link(dve.tensor_tensor(lamp[:, :, :], lamt[:, :, 0, :], lamt[:, :, 1, :], ALU.mult))
            dve.tensor_reduce(lams[:, :], lamp[:, :, :], AX.X, ALU.add).then_inc(lsum_rdy, 1)

            for f in range(NPC):
                dve.wait_ge(mh_rdy, f + 1)
                dve.tensor_tensor(ml[:, f * PIECE:(f + 1) * PIECE], m_acc[f % 2][:, 0:PIECE],
                                  mh[:, f * PIECE:(f + 1) * PIECE].bitcast(F32), ALU.subtract).then_inc(ml_rdy, 1)
                if f == 4:
                    dve.wait_ge(rb_rdy, 1)
                    dve.wait_ge(zeros, 1)
                    dve.wait_ge(consts, 6)
                    link(dve.tensor_tensor(rsel[:, :, :], r_b[:, :].rearrange("p (g q) -> p g q", q=GTOK),
                                           sel[:, :].unsqueeze(1).to_broadcast([P, NG, GTOK]), ALU.mult))
                    link(dve.tensor_reduce(rq[:, 0:NG], rsel[:, :, :], AX.X, ALU.add))
                    dve.tensor_scalar(rq8[:, :], rq[:, :], DH ** -0.5, None, ALU.mult)
                    pairs = rq[:, :].rearrange("p (t g) -> p t g", g=2)
                    for i in range(2):
                        last = dve.tensor_copy(rk[GP * i:GP * i + GP, :], pairs[GP * i:GP * i + GP, :, i])
                    last.then_inc(rk_rdy, 1)
            dve.wait_ge(cb_rdy, 1)
            dve.wait_ge(rb_mm, 1)
            dve.tensor_tensor(diag[:, 0:KD, :], ident[:, :].unsqueeze(1).to_broadcast([P, KD, P]),
                              cbias[:, 2 * NPAIR:].unsqueeze(2).to_broadcast([P, KD, P]), ALU.mult).then_inc(dv_rdy, 1)
            dve.wait_ge(cv_mm, 1)
            dve.tensor_copy(cv_b[:, :], cv_acc).then_inc(cv_rdy, 1)
            dve.wait_ge(cv_rdy, 1)
            dve.wait_ge(lexp_rdy, 1)
            link(dve.scalar_tensor_tensor(neglam[:, :], lame[:, 1:2], L_INIT, lame[:, 0:1], ALU.subtract, ALU.subtract))

            def evacuate(u0, u1):
                for u in range(u0, u1):
                    if is_q(u):
                        continue
                    kind, half, c = uses[u]
                    dve.wait_ge(ring_mm, u + 1)
                    if kind == "qk":
                        g0, g1 = groups(half)
                        t0, t1 = g0 * GTOK, g1 * GTOK
                        dve.scalar_tensor_tensor(kt[:, c - NPAIR, t0:t1], ring[u % 3][:, 0:t1 - t0], cbias[:, c:c + 1],
                                                 r_b[:, t0:t1], ALU.add, ALU.mult).then_inc(kv_ev, 1)
                    else:
                        dve.tensor_tensor(v[:, half, :], ring[u % 3], cv_b[:, :], ALU.add).then_inc(kv_ev, 1)

            def mean_abs(raw, loaded, k):
                dve.wait_ge(loaded, 16)
                link(dve.tensor_reduce(part[:, :], raw, AX.X, ALU.add, apply_absolute_value=True))
                dve.tensor_reduce(psm[:, k:k + 1], part[:, :], AX.X, ALU.add).then_inc(ab_rdy, 1)

            def threshold(k, total):
                dve.wait_ge(ab_mm, k + 1)
                link(dve.tensor_scalar(am[:, k:k + 1], total, 1.0 / (D * HID), 1e-5, ALU.mult, ALU.max))
                link(dve.tensor_scalar(thr[:, k, 0:1], am[:, k:k + 1], 0.7, None, ALU.mult))
                link(dve.tensor_scalar(thr[:, k, 1:2], thr[:, k, 0:1], -1.0, None, ALU.mult))

            def ternary(q, raw, k):
                link(dve.tensor_scalar(q, raw, thr[:, k, 1:2], None, ALU.is_lt))
                return dve.scalar_tensor_tensor(q, raw, thr[:, k, 0:1], q, ALU.is_gt, ALU.subtract)

            evacuate(0, n_first)
            for T in range(NT + 2):
                if T < NT:
                    for i in gps(T):
                        g = 2 * T + i
                        s3 = s_acc[g % 2].rearrange("p (c k) -> p c k", k=GP)
                        dve.wait_ge(s_mm, g + 1)
                        link(dve.tensor_reduce(mx[:, g % 2, :], s3, AX.X, ALU.max))
                        if g >= 3:
                            dve.wait_ge(a_rdy, g - 2)
                        dve.tensor_tensor(e[g % 3][:, :, :], s3, mx[:, g % 2, :].unsqueeze(2).to_broadcast([P, NPAIR, GP]),
                                          ALU.subtract).then_inc(d_rdy, 1)
                if T < 2:
                    evacuate(cut[2 * T], cut[2 * T + 1])
                if T < NT:
                    for i in gps(T):
                        g = 2 * T + i
                        dve.wait_ge(e_rdy, g + 1)
                        link(dve.tensor_reduce(ssum[:, g % 2, :], e[g % 3][:, :, :], AX.X, ALU.add))
                        link(dve.reciprocal(sinv[:, g % 4, :], ssum[:, g % 2, :]))
                        dve.scalar_tensor_tensor(ratio[:, g % 3, :], ssum[:, g % 2, 0:NHP], neglam[:, :],
                                                 sinv[:, g % 4, NHP:], ALU.mult, ALU.mult).then_inc(rat_rdy, 1)
                if T < 2:
                    evacuate(cut[2 * T + 1], cut[2 * T + 2])
                if T >= 2:
                    dve.wait_ge(oth_rdy, T - 1)
                    for i in gps(T - 2):
                        g = 2 * (T - 2) + i
                        for j in range(2):
                            o_ = slice(g * GTOK, (g + 1) * GTOK)
                            last = dve.tensor_tensor(
                                otl[:, 2 * j:2 * j + 2, o_],
                                at_acc[:, (2 * i + j) * P:(2 * i + j + 1) * P].rearrange(
                                    "p (h q) -> p h q", q=GP)[:, :, 0:GTOK],
                                oth[:, 2 * j:2 * j + 2, o_].bitcast(F32), ALU.subtract)
                    last.then_inc(otl_rdy, 1)
                if 1 <= T <= NT:
                    n_gp = len(gps(T - 1))
                    on_ = on[(T - 1) % 2]
                    s0 = 2 * (T - 1) % 4
                    dve.wait_ge(av_mm, T)
                    if T >= 3:
                        dve.wait_ge(ot_mm, T - 2)
                    dve.tensor_tensor(on_[:, 0:n_gp, :, :],
                                      o_ps[:, 0:n_gp, 0:NHP * DH].rearrange("p g (j d) -> p g j d", d=DH),
                                      sinv[:, s0:s0 + n_gp, 0:NHP].unsqueeze(3).to_broadcast([P, n_gp, NHP, DH]),
                                      ALU.mult).then_inc(on_rdy, 1)
                    dve.wait_ge(sq_rdy, T)
                    m = 32 * n_gp
                    link(dve.tensor_reduce(ms[:, 0:m], osq[:, 0:n_gp].rearrange("p g j (c d) -> p (g j c) d", d=RMSW),
                                           AX.X, ALU.add))
                    link(dve.tensor_scalar(nx[:, 0:m], ms[:, 0:m], 1.0 / RMSW / (1 - L_INIT) ** 2,
                                           RMS_EPS / (1 - L_INIT) ** 2, ALU.mult, ALU.add))
                    if T >= 2:
                        dve.wait_ge(on2_rdy, T - 1)
                    rsqrt(ny[:, 0:m], nx[:, 0:m], nt_[:, 0:m]).then_inc(rms_rdy, 1)
                if T == 2:
                    mean_abs(fc_raw[:, :, :].rearrange("p k f -> p (k f)").rearrange("p (c f) -> p c f", f=D), ld_fc, 0)
                if T == 3:
                    threshold(0, bank[7][:, 0:1])
                if 3 <= T <= 6:
                    ternary(qfc[:, T - 3, :], fc_raw[:, T - 3, :], 0).then_inc(qfc_rdy, 1)
                if T == NT:
                    mean_abs(proj_raw[:, :, :], ld_proj, 1)
            threshold(1, bank[7][:, 0:1])
            dve.wait_ge(qfc_rdy, 4)

            def z_lo(i):
                dve.wait_ge(zth_rdy, i + 1)
                dve.tensor_tensor(ztl[:, :, i * P:(i + 1) * P], zt_acc[i % 2].rearrange("p (k t) -> p k t", t=P),
                                  zth[:, :, i * P:(i + 1) * P], ALU.subtract).then_inc(ztl_rdy, 1)

            for i in range(TT):
                dve.wait_ge(wo_mm, i + 1)
                dve.tensor_tensor(h[:, i, :], h[:, i, :], wo_acc[i % 2], ALU.add).then_inc(h1_rdy, 1)
                dve.wait_ge(h1_rdy, i + 1)
                link(dve.bn_stats(bnst[:, i, :], h[:, i, :]))
                link(dve.bn_aggr(stat2[:, i, :], bnst[:, i, :]))
                link(dve.tensor_scalar(nx[:, 0:1], stat2[:, i, 1:2], Z_SCALE ** -2, LN_EPS * Z_SCALE ** -2,
                                       ALU.mult, ALU.add))
                link(rsqrt(ny[:, 0:1], nx[:, 0:1], nt_[:, 0:1]))
                if i >= 2:
                    dve.wait_ge(zt_mm, i - 1)
                dve.tensor_scalar(z[i % 2][:, :], h[:, i, :], stat2[:, i, 0:1], ny[:, 0:1].bitcast(F32),
                                  ALU.subtract, ALU.mult).then_inc(z_rdy, 1)
                dve.wait_ge(z_rdy, i + 1)
                if i >= 1:
                    z_lo(i - 1)
            z_lo(TT - 1)

            def g_lo(k):
                half, c = divmod(k, HC)
                t0, t1 = FFN_TILES[half]
                dve.wait_ge(gh_rdy, k + 1)
                dve.tensor_tensor(gl[:, c, t0 * P:t1 * P], squ[k % 2][:, 0:(t1 - t0) * P], gh[:, c, t0 * P:t1 * P],
                                  ALU.subtract).then_inc(gl_rdy, 1)

            for k in range(2 * HC):
                g_lo(k)
                if k < HC:
                    ternary(qproj[:, k, :], proj_raw[:, k, :], 1).then_inc(qproj_rdy, 1)
            link(dve.tensor_scalar(sout[:, :], am[:, 0:1], am[:, 0:1], am[:, 1:2], ALU.mult, ALU.mult))
            link(dve.tensor_scalar(sout[:, :], sout[:, :], H_SCALE ** -2, None, ALU.mult))
            for i in range(TT):
                dve.wait_ge(pj_mm, i + 1)
                if i >= 2:
                    dve.wait_ge(st_out[i % 2], 16 * (i // 2))
                dve.scalar_tensor_tensor(orow[i % 2][:, :], pj_acc[i % 2], sout[:, :], h[:, i, :],
                                         ALU.mult, ALU.add).then_inc(o_rdy, 1)

        @block.tensor
        def _(pe):
            def mm(o, l, r, start, stop):
                return pe.matmul(o, l, r, start=start, stop=stop, skip_group_check=True)

            pe.wait_ge(consts, 1)
            pe.wait_ge(ld_w, 32)
            for k in range(KD):
                last = mm(mean_acc[:, 0:FW], mean_w[:, :], wpos[:, k, :], k == 0, k == KD - 1)
            last.then_inc(mean_rdy, 1)
            pe.wait_ge(ld_x, 16)
            for i in range(TT):
                if i >= 2:
                    pe.wait_ge(h_ev, i - 1)
                mm(h_acc[i % 2], pt[:, i * P:(i + 1) * P], wcol[:, :], True, True).then_inc(h_mm, 1)

            def transpose_piece(f):
                pe.wait_ge(mt_rdy, f + 1)
                if f >= 2:
                    pe.wait_ge(ml_rdy, f - 1)
                for c in range(2):
                    last = pe.transpose(m_acc[f % 2][:, c * P:(c + 1) * P], mt[:, 2 * f + c, 0:P], ident[:, :])
                last.then_inc(tr_mm, 1)

            pe.wait_ge(wc_rdy, 1)
            pe.wait_ge(consts, 3)
            for f in range(NPC):
                pe.wait_ge(ld_qkv[f], 16)
                if f >= 2:
                    pe.wait_ge(mt_rdy, f - 1)
                for c in range(2):
                    for k in range(KD):
                        last = mm(fold_acc[f % 2][:, c * FWS:c * FWS + FW], wqkv_s[:, f, k, c * P:(c + 1) * P],
                                  wc[:, k, :], k == 0, k == KD - 1)
                last.then_inc(fold_mm, 1)
                if f >= 1:
                    transpose_piece(f - 1)
                if f == 3:
                    pe.wait_ge(dg_rdy, 1)
                    dg = diag[:, :, :].rearrange("p t q -> p (t q)")
                    for i in range(2):
                        last = mm(rb_acc[i][:, 0:320], ones[:, :], dg[:, 320 * i:320 * i + 320], True, True)
                    last.then_inc(rb_mm, 1)
            transpose_piece(NPC - 1)
            pe.wait_ge(dv_rdy, 1)
            mm(cv_acc, ones[:, :], diag[:, 0:KD, :].rearrange("p t q -> p (t q)"), True, True).then_inc(cv_mm, 1)

            def project(u0, u1):
                for u in range(u0, u1):
                    kind, half, c = uses[u]
                    if u >= 3:
                        pe.wait_ge(*evacuated(u - 3))
                    if kind == "qk":
                        g0, g1 = groups(half)
                        o = ring[u % 3][:, 0:(g1 - g0) * GTOK]
                        w = slice(c * P, (c + 1) * P)
                        mm(o, mh[:, w], ph[:, g0:g1, 0:GTOK], True, False)
                        mm(o, mh[:, w], pl[:, g0:g1, 0:GTOK], False, False)
                        last = mm(o, ml[:, w], ph[:, g0:g1, 0:GTOK], False, True)
                    else:
                        T = half
                        o = ring[u % 3]
                        xh = ph[:, 2 * T:2 * T + 2, :].rearrange("p g q -> p (g q)")
                        xl = pl[:, 2 * T:2 * T + 2, :].rearrange("p g q -> p (g q)")
                        mm(o, xh, mh[:, 4 * D:], True, False)
                        mm(o, xh, ml[:, 4 * D:], False, False)
                        last = mm(o, xl, mh[:, 4 * D:], False, True)
                    last.then_inc(ring_mm, 1)

            pe.wait_ge(zeros, 1)
            pe.wait_ge(pl_rdy, 1)
            pe.wait_ge(ml_rdy, NPC)
            pe.wait_ge(rb_rdy, 1)
            project(0, n_first)
            pe.wait_ge(consts, 7)
            pe.wait_ge(cv_rdy, 1)
            for T in range(NT + 2):
                if T < NT:
                    for i in gps(T):
                        g = 2 * T + i
                        if i == 0:
                            u = (n_first if g < HALF_G[0] else n_uses) - 1
                            nq = sum(is_q(w) for w in range(u + 1))
                            pe.wait_ge(q_ev, nq)
                            pe.wait_ge(kv_ev, u + 1 - nq)
                        if g >= 2:
                            pe.wait_ge(d_rdy, g - 1)
                        mm(s_acc[g % 2], ident_b[:, :], mask[:, :, :].rearrange("p c k -> p (c k)"), True, False)
                        for c in range(NPAIR):
                            last = mm(s_acc[g % 2][:, c * GP:c * GP + GTOK],
                                      qbd[:, c, g, :, :].rearrange("p h q -> p (h q)"),
                                      kt[:, c, g * GTOK:(g + 1) * GTOK], False, c == NPAIR - 1)
                        last.then_inc(s_mm, 1)
                if T < 2:
                    project(cut[2 * T], cut[2 * T + 1])
                if 1 <= T <= NT:
                    pe.wait_ge(a_rdy, min(2 * T, NG))
                    if T >= 3:
                        pe.wait_ge(otl_rdy, T - 2)
                    for j in range(NHP):
                        last = pe.transpose(at_acc[:, j * P:(j + 1) * P],
                                            a[(T - 1) % 2][:, j, :, :].rearrange("p g k -> p (g k)"), ident[:, :])
                    last.then_inc(at_mm, 1)
                if T < 2:
                    project(cut[2 * T + 1], cut[2 * T + 2])
                if 1 <= T <= NT:
                    pe.wait_ge(at_rdy, T)
                    if T == 1:
                        pe.wait_ge(kv_ev, NPAIR + 3)
                    if T == 4:
                        pe.wait_ge(kv_ev, n_kv)
                    if T >= 2:
                        pe.wait_ge(on_rdy, T - 1)
                    for i in gps(T - 1):
                        r0 = GP * i
                        for j in range(NHP):
                            for s in range(2):
                                last = mm(o_ps[GP * s:GP * s + GP, i, j * DH:(j + 1) * DH],
                                          ats[(T - 1) % 2][r0:r0 + GTOK, j, s, :],
                                          v[r0:r0 + GTOK, T - 1, (2 * j + s) * DH:(2 * j + s + 1) * DH], True, True)
                    last.then_inc(av_mm, 1)
                if T >= 2:
                    pe.wait_ge(on2_rdy, T - 1)
                    if T - 1 <= NT:
                        pe.wait_ge(at_rdy, min(T, NT))
                    for i in gps(T - 2):
                        for j in range(2):
                            last = pe.transpose(at_acc[:, (2 * i + j) * P:(2 * i + j + 1) * P],
                                                on[T % 2][:, i, 2 * j:2 * j + 2, :].rearrange("p j d -> p (j d)"),
                                                ident[:, :])
                    last.then_inc(ot_mm, 1)
                if T == 3:
                    pe.wait_ge(ab_rdy, 1)
                    mm(bank[7][:, 0:1], ones[:, :], psm[:, 0:1], True, True).then_inc(ab_mm, 1)
            pe.wait_ge(ab_rdy, 2)
            mm(bank[7][:, 0:1], ones[:, :], psm[:, 1:2], True, True).then_inc(ab_mm, 1)

            pe.wait_ge(wos_rdy, 1)

            def transpose_z(i):
                pe.wait_ge(z_rdy, i + 1)
                if i >= 2:
                    pe.wait_ge(ztl_rdy, i - 1)
                for k in range(KD):
                    last = pe.transpose(zt_acc[i % 2][:, k * P:(k + 1) * P], z[i % 2][:, k * P:(k + 1) * P], ident[:, :])
                last.then_inc(zt_mm, 1)

            for i in range(TT):
                t = slice(i * P, (i + 1) * P)
                pe.wait_ge(otl_rdy, min(NT, -(-(i + 1) * P // (2 * GTOK))))
                if i >= 2:
                    pe.wait_ge(h1_rdy, i - 1)
                for k in range(KD):
                    mm(wo_acc[i % 2], oth[:, k, t], woh[:, k, :], k == 0, False)
                    mm(wo_acc[i % 2], oth[:, k, t], wol[:, k, :], False, False)
                    last = mm(wo_acc[i % 2], otl[:, k, t], woh[:, k, :], False, k == KD - 1)
                last.then_inc(wo_mm, 1)
                if i >= 1:
                    transpose_z(i - 1)
            transpose_z(TT - 1)

            pe.wait_ge(qfc_rdy, KD)
            for half in range(2):
                t0, t1 = FFN_TILES[half]
                t = slice(t0 * P, t1 * P)
                pe.wait_ge(ztl_rdy, t1)
                for c in range(HC):
                    u = half * HC + c
                    if u >= 2:
                        pe.wait_ge(rel_rdy, u - 1)
                    for k in range(KD):
                        w = qfc[:, k, c * P:(c + 1) * P]
                        mm(fc_acc[u % 2][:, 0:(t1 - t0) * P], w, zth[:, k, t], k == 0, False)
                        last = mm(fc_acc[u % 2][:, 0:(t1 - t0) * P], w, ztl[:, k, t], False, k == KD - 1)
                    last.then_inc(fc_mm, 1)
            pe.wait_ge(qproj_rdy, HC)
            for i in range(TT):
                t = slice(i * P, (i + 1) * P)
                pe.wait_ge(gl_rdy, HC if i < FFN_TILES[0][1] else 2 * HC)
                if i >= 2:
                    pe.wait_ge(o_rdy, i - 1)
                for c in range(HC):
                    mm(pj_acc[i % 2], gh[:, c, t], qproj[:, c, :], c == 0, False)
                    last = mm(pj_acc[i % 2], gl[:, c, t], qproj[:, c, :], False, c == HC - 1)
                last.then_inc(pj_mm, 1)


def kernel(x, L0_tok_W, L0_tok_b, L0_attn_l_q1, L0_attn_l_k1, L0_attn_l_q2, L0_attn_l_k2, L0_attn_wq, L0_attn_wk,
           L0_attn_wv, L0_attn_wo, L0_ffn_w_fc, L0_ffn_w_proj):
    import concourse.bacc as bacc
    import numpy as np
    from concourse.bass_utils import run_bass_kernel_spmd

    f = np.ascontiguousarray
    xs = np.asarray(x)[:, :, 0]
    patches = np.stack([xs[:, STRIDE * n:STRIDE * n + P] for n in range(NPATCH)], axis=1)
    W, bias = np.asarray(L0_tok_W), np.asarray(L0_tok_b)
    wb = np.concatenate([W, bias[:, None]], axis=1)
    wqkv = np.concatenate([np.asarray(L0_attn_wq), np.asarray(L0_attn_wk), np.asarray(L0_attn_wv)])
    wo = np.asarray(L0_attn_wo)
    arrays = {
        "xT": f(patches.reshape(TOK, P).T),
        "w_pos": f(wb.reshape(KD, P, FW).transpose(1, 0, 2)),
        "w_col": f(W.T),
        "b": f(bias),
        "lam": f(np.stack([np.asarray(t) for t in (L0_attn_l_q1, L0_attn_l_k1, L0_attn_l_q2, L0_attn_l_k2)])
                 .reshape(2, 2, NH)),
        "wqkv": f(wqkv.reshape(NPC, PIECE, KD, P).transpose(0, 3, 2, 1)),
        "wo": f(wo.T.reshape(2, 2, 2, DH, D).transpose(1, 3, 0, 2, 4).reshape(P, KD, D)),
        "w_fc": f(np.asarray(L0_ffn_w_fc).reshape(HID, KD, P).transpose(2, 1, 0)),
        "w_proj": f(np.asarray(L0_ffn_w_proj).reshape(D, HC, P).transpose(2, 1, 0)),
    }
    nc = bacc.Bacc("TRN2", target_bir_lowering=False, num_devices=1)
    args = [nc.dram_tensor(n, t.shape, F32, kind="ExternalInput").ap() for n, t in arrays.items()]
    out = nc.dram_tensor("out", (TT, P, D), F32, kind="ExternalOutput").ap()
    audio_block(nc, *args, out)
    r = run_bass_kernel_spmd(nc, [arrays], core_ids=[0])
    return r.results[0]["out"].reshape(NB, NPATCH, D)
```

```python
import math
from contextlib import ExitStack

import concourse.bass as bass
from concourse import mybir

F32 = mybir.dt.float32
F32R = mybir.dt.float32r
F16 = mybir.dt.float16
BF16 = mybir.dt.bfloat16
I32 = mybir.dt.int32
ALU = mybir.AluOpType
ACT = mybir.ActivationFunctionType
AX = mybir.AxisListType

P = 128
NB, NPATCH, STRIDE = 64, 10, 64
D, NH, DH = 512, 8, 64
HID = 1280
KD = D // P
HC = HID // P
TOK = NB * NPATCH
TT = TOK // P
GTOK = 6 * NPATCH
GP = 64
NG = -(-TOK // GTOK)
NT = -(-NG // 2)
TOKG = NG * GTOK
NPAIR = 2 * NH // 2
NHP = NH // 2
QKV = 5 * D
PIECE = 256
NPC = QKV // PIECE
FW = P + 1
FWS = 132
L_INIT = 0.8 - 0.6 * math.exp(-0.3 * 1)
LN_EPS, RMS_EPS = 1e-5, 1e-6
RMSW = 8
BATCHES = ((0, 2), (2, 4), (4, 6))
BATCH_G = 4
MASKED = -1.0e30
Z_SCALE = 2.0 ** 11
H_SCALE = 2.0 ** -2
HALF_G = (6, NG - 6)
FFN_TILES = ((0, 2), (2, TT))
QK_ORDER = [c for j in range(NPAIR) for c in (j, NPAIR + j)]


def rsqrt_guess(dve, link, y, x):
    link(dve.tensor_scalar(y, x.bitcast(I32), 1, None, ALU.logical_shift_right))
    return dve.tensor_scalar(y, y, -1.0, float(0x5F3759DF), ALU.mult, ALU.add)


def audio_block(nc, xT, w_pos, w_col, b, lam, wqkv, wo, w_fc, w_proj, out):
    with ExitStack() as ctx:
        def at(name, shape, dtype, offset):
            return nc.alloc_sbuf_tensor_at(name, shape, dtype, offset=offset)

        def sem(name):
            return ctx.enter_context(nc.semaphore(name))

        top = [(nc.sbuf_base + 31) // 32 * 32]

        def region(size):
            start = top[0]
            top[0] += (size + 31) // 32 * 32
            return start

        ones = at("ones", [P, P], F32, region(512))
        mean_w = at("mean_w", [P, P], F32, region(512))
        ident = at("ident", [P, P], F32, region(512))
        ident_b = at("ident_b", [P, P], BF16, region(256))
        mask = at("mask", [P, NPAIR, GP], BF16, region(1024))
        cv_b = at("cv_b", [P, D], F32, region(2048))
        r_b = at("r_b", [P, TOKG], F32, region(4 * TOKG))
        ph = at("ph", [P, 2 * NT, GP], F32R, region(3072))
        pl = at("pl", [P, 2 * NT, GP], F32R, region(3072))
        h = at("h", [P, TT, D], F32, region(4 * TT * D))
        sel = at("sel", [P, GTOK], F32, region(4 * GTOK))
        lamt = at("lamt", [P, 2, 2, NH], F32, region(128))
        lamp = at("lamp", [P, 2, NH], F32, region(64))
        lams = at("lams", [P, 2], F32, region(8))
        lame = at("lame", [P, 2], F32, region(8))
        neglam = at("neglam", [P, 1], F32, region(4))
        bnst = at("bnst", [P, TT, 6], F32, region(120))
        stat = at("stat", [P, TT, 2], F32, region(40))
        stat2 = at("stat2", [P, TT, 2], F32, region(40))
        rtok = at("rtok", [P, TT], F32, region(20))
        rtok2 = at("rtok2", [P, TT], F32, region(20))
        rq = at("rq", [P, 2 * NT], F32, region(48))
        rq8 = at("rq8", [P, 2 * NT], F32, region(48))
        rk = at("rk", [P, NT], F32, region(24))
        nx = at("nx", [P, 2, BATCH_G, NHP, RMSW], F32, region(1024))
        nt = at("nt", [P, 2, BATCH_G, NHP, RMSW], F32, region(1024))
        ny = at("ny", [P, 2, BATCH_G, NHP, RMSW], I32, region(1024))
        linv = at("linv", [P, TT], F32, region(20))
        lshift = at("lshift", [P, TT], F32, region(20))
        lx = at("lx", [P, TT], F32, region(20))
        lt = at("lt", [P, TT], F32, region(20))
        ly = at("ly", [P, TT], I32, region(20))
        mx = at("mx", [P, 2, NPAIR], F32, region(64))
        ssum = at("ssum", [P, 2, NPAIR], F32, region(64))
        sinv = at("sinv", [P, NG, NPAIR], F32, region(4 * NG * NPAIR))
        sinv2 = at("sinv2", [P, BATCH_G, NHP], F32, region(96))
        ratio = at("ratio", [P, 3, NHP], F32, region(48))
        ms = at("ms", [P, 2 * NT, NHP, RMSW], F32, region(1536))
        part = at("part", [P, 2, HC], F32, region(80))
        psm = at("psm", [P, 2], F32, region(8))
        am = at("am", [P, 2], F32, region(8))
        thr = at("thr", [P, 2], F32, region(8))
        sout = at("sout", [P, 1], F32, region(4))

        ra = region(4 * KD * QKV)
        wqkv_s = at("wqkv_s", [P, NPC, KD, PIECE], F32, ra)
        fc_raw = at("fc_raw", [P, KD, HID], F32, ra)
        proj_raw = at("proj_raw", [P, HC, D], F32, ra + 4 * KD * HID)

        rqd = region(4 * NPAIR * NG * 2 * GP)
        qbd = at("qbd", [P, NG, NPAIR, 2, GP], F32, rqd)
        zth = at("zth", [P, KD, TOK], F16, rqd)
        ztl = at("ztl", [P, KD, TOK], F16, rqd + 5120)
        gh = at("gh", [P, HC, TOK], F16, rqd + 10240)
        gl = at("gl", [P, HC, TOK], F16, rqd + 23040)
        rel = [at(f"rel{i}", [P, 384], F32, rqd + 35840 + 1536 * i) for i in range(2)]
        squ = [at(f"squ{i}", [P, 384], F32, rqd + 38912 + 1536 * i) for i in range(2)]

        rkt = region(4 * NPAIR * TOKG)
        kt = at("kt", [P, NPAIR, TOKG], F32, rkt)
        z = [at(f"z{i}", [P, D], F32, rkt + 2048 * i) for i in range(3)]
        orow = [at(f"orow{i}", [P, D], F32, rkt + 6144 + 2048 * i) for i in range(2)]

        rv = region(4 * NT * D)
        v = at("v", [P, NT, D], F32, rv)
        on = at("on", [P, NT, 2, NHP, DH], F32, rv)

        rm = region(4 * (QKV // P) * FW)
        mt = at("mt", [P, QKV // P, FW], F32, rm)
        wo_s = at("wo_s", [P, KD, D], F32, rm)

        rmm = region(max(8 * QKV, 4 * NHP * TOKG + 2 * HC * D))
        mh = at("mh", [P, QKV], F32R, rmm)
        ml = at("ml", [P, QKV], F32R, rmm + 4 * QKV)
        ot = at("ot", [P, NHP, TOKG], F32, rmm)
        qproj = at("qproj", [P, HC, D], F16, rmm + 4 * NHP * TOKG)

        qfc = at("qfc", [P, KD, HID], F16, region(2 * KD * HID))

        rw = region(18432)
        pt = at("pt", [P, TOK], F32, rw)
        wcol = at("wcol", [P, D], F32, rw + 2560)
        wpos = at("wpos", [P, KD, FW], F32, rw + 4608)
        wc = at("wc", [P, KD, FW], F32, rw + 6688)
        b_b = at("b_b", [P, D], F32, rw + 8768)
        diag = at("diag", [P, TT, P], F32, rw + 10816)
        rsel = at("rsel", [P, NG, GTOK], F32, rw + 10816 + 2560)
        e = [at(f"e{i}", [P, NPAIR, GP], F32, rw + 2048 * i) for i in range(3)]
        a = [at(f"a{i}", [P, NHP, 2, GP], F32, rw + 6144 + 2048 * i) for i in range(2)]
        ats = [at(f"ats{i}", [P, NHP, 2, GP], F32, rw + 10240 + 2048 * i) for i in range(2)]
        osq = [at(f"osq{i}", [P, 2, NHP, DH], F32, rw + 14336 + 2048 * i) for i in range(2)]
        assert top[0] <= nc.sbuf_usable_end, (top[0], nc.sbuf_usable_end)

        bank = [ctx.enter_context(nc.psum_tensor(f"bank{i}", [P, 512], F32)) for i in range(3)]
        o_ps = ctx.enter_context(nc.psum_tensor("o_ps", [P, 2, 512], F32))
        bank += [o_ps[:, 0, :], o_ps[:, 1, :]]
        bank += [ctx.enter_context(nc.psum_tensor(f"bank{i}", [P, 512], F32)) for i in range(5, 8)]
        bank = [x[:, :] for x in bank]
        h_acc = (bank[0], bank[5], bank[7], bank[3], bank[4])
        fold_acc = (bank[1], bank[2])
        m_acc = (bank[3], bank[4], bank[0], bank[5])
        rb_acc = (bank[6], bank[7])
        cv_acc = bank[0]
        mean_acc = bank[6]
        ring = bank[5:8]
        s_acc = bank[0:2]
        at_acc = bank[2]
        wo_acc = bank[5:7]
        ot_acc = (bank[7], bank[1])
        zt_acc = (bank[2], bank[7])
        fc_acc = bank[0:2]
        pj_acc = (bank[3], bank[4])
        abs_acc = (bank[7][:, 0:1], bank[3][:, 0:1])

        ld_x, ld_wpos, ld_wcol, ld_lam, ld_b, ld_wo = sem("ld_x"), sem("ld_wpos"), sem("ld_wcol"), sem("ld_lam"), sem("ld_b"), sem("ld_wo")
        ld_qkv = [sem(f"ld_qkv{f}") for f in range(NPC)]
        ld_fc, ld_proj = sem("ld_fc"), sem("ld_proj")
        st_out = [sem(f"st_out{i}") for i in range(2)]
        consts = sem("consts")
        pchain = sem("pchain")
        zeros = sem("zeros")
        ph_rdy, pl_rdy = sem("ph_rdy"), sem("pl_rdy")
        mean_rdy, wc_rdy = sem("mean_rdy"), sem("wc_rdy")
        h_mm, h_ev = sem("h_mm"), sem("h_ev")
        fold_mm, mt_rdy = sem("fold_mm"), sem("mt_rdy")
        tr_mm, mh_rdy, ml_rdy = sem("tr_mm"), sem("mh_rdy"), sem("ml_rdy")
        dg_rdy, rb_mm, rb_rdy, rk_rdy = sem("dg_rdy"), sem("rb_mm"), sem("rb_rdy"), sem("rk_rdy")
        dv_rdy, cv_mm, cv_rdy = sem("dv_rdy"), sem("cv_mm"), sem("cv_rdy")
        ring_mm = sem("ring_mm")
        q_ev = sem("q_ev")
        kv_ev = sem("kv_ev")
        s_mm, d_rdy, e_rdy, rat_rdy, a_rdy = sem("s_mm"), sem("d_rdy"), sem("e_rdy"), sem("rat_rdy"), sem("a_rdy")
        at_mm, at_rdy, av_mm, on_rdy = sem("at_mm"), sem("at_rdy"), sem("av_mm"), sem("on_rdy")
        ms_rdy, msq_rdy, root_rdy, rms_rdy, on2_rdy = (sem("ms_rdy"), sem("msq_rdy"), sem("root_rdy"), sem("rms_rdy"),
                                                       sem("on2_rdy"))
        ot_mm, ot_rdy, zt_mm, zth_rdy, ztl_rdy = (sem("ot_mm"), sem("ot_rdy"), sem("zt_mm"), sem("zth_rdy"),
                                                  sem("ztl_rdy"))
        var_rdy, lroot_rdy, shift_rdy = sem("var_rdy"), sem("lroot_rdy"), sem("shift_rdy")
        lsum_rdy, lexp_rdy = sem("lsum_rdy"), sem("lexp_rdy")
        abs_rdy, ab_rdy, ab_mm = sem("abs_rdy"), sem("ab_rdy"), sem("ab_mm")
        thr_rdy = sem("thr_rdy")
        qfc_rdy, qproj_rdy = sem("qfc_rdy"), sem("qproj_rdy")
        wo_mm, h1_rdy, z_rdy = sem("wo_mm"), sem("h1_rdy"), sem("z_rdy")
        fc_mm, rel_rdy, squ_rdy, gh_rdy, gl_rdy = (sem("fc_mm"), sem("rel_rdy"), sem("squ_rdy"), sem("gh_rdy"),
                                                   sem("gl_rdy"))
        pj_mm, o_rdy = sem("pj_mm"), sem("o_rdy")
        vchain = sem("vchain")
        achain = sem("achain")

        uses = [("qk", 0, c) for c in QK_ORDER] + [("v", T, 0) for T in range(3)]
        n_first = len(uses)
        uses += [("qk", 1, c) for c in QK_ORDER] + [("v", T, 0) for T in range(3, NT)]
        n_uses = len(uses)
        n_second = n_uses - (NT - 3)
        fill = [n_first + (n_second - n_first) * i // HALF_G[0] for i in range(HALF_G[0] + 1)]
        fill += range(n_second + 1, n_uses + 1)
        fill += [n_uses] * (NG + 1 - len(fill))

        def is_q(u):
            return uses[u][0] == "qk" and uses[u][2] < NPAIR

        def evacuated(u):
            n = sum(is_q(w) for w in range(u + 1))
            return (q_ev, n) if is_q(u) else (kv_ev, u + 1 - n)

        def groups(half):
            return (0, HALF_G[0]) if half == 0 else (HALF_G[0], NG)

        def gps(T):
            return range(min(2, NG - 2 * T))

        def pair_of_step(n):
            return (n - 4) // 2 if n >= 4 and n % 2 == 0 else None

        def batch_groups(b):
            return range(2 * BATCHES[b][0], min(2 * BATCHES[b][1], NG))

        n_kv = n_uses - NPAIR * 2

        block = ctx.enter_context(nc.Block())

        @block.sync
        def _(sp):
            sp.dma_start(wpos[:, :, :], w_pos).then_inc(ld_wpos, 16)
            sp.dma_start(pt[:, :], xT).then_inc(ld_x, 16)
            sp.dma_start(wcol[:, :], w_col).then_inc(ld_wcol, 16)
            sp.dma_start(wqkv_s[:, 0, :, :], wqkv[0]).then_inc(ld_qkv[0], 16)
            sp.dma_start(b_b[:, :], b.partition_broadcast(P)).then_inc(ld_b, 16)
            for f in range(1, NPC):
                sp.dma_start(wqkv_s[:, f, :, :], wqkv[f]).then_inc(ld_qkv[f], 16)
            sp.dma_start(lamt[:, :, :, :], lam.partition_broadcast(P)).then_inc(ld_lam, 16)
            sp.wait_ge(fold_mm, NPC // 2)
            sp.dma_start(fc_raw[:, :, :], w_fc).then_inc(ld_fc, 16)
            sp.wait_ge(fold_mm, NPC)
            sp.dma_start(proj_raw[:, :, :], w_proj).then_inc(ld_proj, 16)
            sp.wait_ge(q_ev, 2 * NPAIR)
            sp.wait_ge(kv_ev, n_kv)
            sp.dma_start(wo_s[:, :, :], wo).then_inc(ld_wo, 16)
            for i in range(TT):
                sp.wait_ge(o_rdy, i + 1)
                sp.dma_start(out[i], orow[i % 2][:, :]).then_inc(st_out[i % 2], 16)
            for i in range(2):
                sp.wait_ge(st_out[i], 16 * len(range(i, TT, 2)))

        @block.gpsimd
        def _(pool):
            n = [0]

            def link(ins):
                n[0] += 1
                ins.then_inc(pchain, 1)
                pool.wait_ge(pchain, n[0])

            pool.memset(mean_w[:, :], 1.0 / D).then_inc(consts, 1)
            pool.memset(ones[:, :], 1.0).then_inc(consts, 1)
            link(pool.memset(ident[:, :], 0.0))
            pool.affine_select(out=ident[:, :], in_=ident[:, :], compare_op=ALU.not_equal, fill=1.0, base=0,
                               pattern=[[-1, P]], channel_multiplier=1).then_inc(consts, 1)
            for t in (ph, pl):
                pool.memset(t[:, :, GTOK:].bitcast(F32), 0.0)
                pool.memset(t[:, NG - 1, TOK - (NG - 1) * GTOK:GTOK].bitcast(F32), 0.0)
                pool.memset(t[:, NG, 0:GTOK].bitcast(F32), 0.0)
            pool.memset(rq[:, NG:], 0.0)
            pool.memset(r_b[:, TOK:], 0.0).then_inc(zeros, 1)
            pool.wait_ge(consts, 3)
            pool.wait_ge(zeros, 1)
            pool.tensor_copy(ident_b[:, :], ident[:, :]).then_inc(consts, 1)
            for half in range(2):
                s = GP * half
                pool.wait_ge(consts, 4 + half)
                pool.tensor_copy(sel[s:s + GP, :], ident[s:s + GP, s:s + GTOK]).then_inc(consts, 1)
            pool.wait_ge(consts, 6)
            link(pool.memset(mask[:, :, 0:GTOK], 0.0))
            link(pool.memset(mask[:, :, GTOK:], MASKED))
            for half in range(2):
                s = GP * half
                m = mask[s:s + GP, :, 0:GTOK]
                link(pool.affine_select(out=m, in_=m, compare_op=ALU.is_ge, fill=MASKED, base=NPATCH - 1,
                                        pattern=[[0, NPAIR], [NPATCH, 6], [0, NPATCH]], channel_multiplier=-1))
                last = pool.affine_select(out=m, in_=m, compare_op=ALU.is_ge, fill=MASKED, base=0,
                                          pattern=[[0, NPAIR], [-1, GTOK]], channel_multiplier=1)
                if half == 0:
                    link(last)
            last.then_inc(consts, 1)
            pool.wait_ge(consts, 7)

            def clear_blocks(g0, g1):
                blocks = qbd[:, g0:g1, :, :, :].rearrange("p g c a q -> p (g c) (a q)")
                link(pool.memset(blocks[0:GP, :, GTOK:], 0.0))
                link(pool.memset(blocks[GP:P, :, 0:GP], 0.0))
                pool.memset(blocks[GP:P, :, GP + GTOK:], 0.0).then_inc(zeros, 1)

            clear_blocks(0, HALF_G[0])
            pool.wait_ge(zeros, 2)
            clear_blocks(HALF_G[0], NG)
            pool.wait_ge(zeros, 3)

            def combine(g):
                T, i = divmod(g, 2)
                eg, ag = e[g % 3], a[T % 2]
                if T >= 2 and i == 0:
                    pool.wait_ge(at_mm, T - 1)
                pool.wait_ge(rat_rdy, g + 1)
                link(pool.tensor_tensor(eg[:, NHP:, :], eg[:, NHP:, :],
                                        ratio[:, g % 3, :].unsqueeze(2).to_broadcast([P, NHP, GP]), ALU.mult))
                pool.tensor_tensor(ag[:, :, i, :], eg[:, NHP:, :], eg[:, 0:NHP, :], ALU.add).then_inc(a_rdy, 1)

            def rms_roots():
                pool.wait_ge(msq_rdy, 1)
                f, t = ny[:, 0].bitcast(F32), nt[:, 0]
                for _ in range(3):
                    link(pool.tensor_tensor(t, f, f, ALU.mult))
                    link(pool.tensor_tensor(t, t, nx[:, 0], ALU.mult))
                    link(pool.tensor_scalar(t, t, -0.5, 1.5, ALU.mult, ALU.add))
                    link(pool.tensor_tensor(f, f, t, ALU.mult))
                link(pool.tensor_tensor(f, f, sinv[:, 0:BATCH_G, 0:NHP].unsqueeze(3)
                                        .to_broadcast([P, BATCH_G, NHP, RMSW]), ALU.mult))

            def normalize(T):
                n_gp = len(gps(T))
                w = on[:, T, 0:n_gp].rearrange("p g j (c d) -> p (g j c) d", d=RMSW)
                g0 = 2 * (T % 2)
                y = ny[:, T // 2 % 2, g0:g0 + n_gp].bitcast(F32).rearrange("p g j c -> p (g j c)")
                pool.tensor_tensor(w, w, y.unsqueeze(2).to_broadcast([P, 32 * n_gp, RMSW]),
                                   ALU.mult).then_inc(on2_rdy, 1)

            for g in range(NG):
                combine(g)
                if g == 7:
                    rms_roots()
                if g == 9:
                    normalize(0)
                    normalize(1)
            for b in (1, 2):
                pool.wait_ge(rms_rdy, b)
                for T in range(*BATCHES[b]):
                    normalize(T)
            for k in range(2 * HC):
                n_tok = P * (FFN_TILES[k // HC][1] - FFN_TILES[k // HC][0])
                pool.wait_ge(rel_rdy, k + 1)
                if k >= 2:
                    pool.wait_ge(gl_rdy, k - 1)
                r_ = rel[k % 2][:, 0:n_tok]
                pool.tensor_tensor(squ[k % 2][:, 0:n_tok], r_, r_, ALU.mult).then_inc(squ_rdy, 1)

        @block.scalar
        def _(act):
            n = [0]

            def link(ins):
                n[0] += 1
                ins.then_inc(achain, 1)
                act.wait_ge(achain, n[0])

            full = (NG - 1)
            rest = TOK - full * GTOK
            act.wait_ge(ld_x, 16)
            act.activation(ph[:, 0:full, 0:GTOK], pt[:, 0:full * GTOK].rearrange("p (g q) -> p g q", q=GTOK), ACT.Copy)
            act.activation(ph[:, full, 0:rest], pt[:, full * GTOK:], ACT.Copy).then_inc(ph_rdy, 1)

            def m_hi(f):
                act.wait_ge(tr_mm, f + 1)
                act.activation(mh[:, f * PIECE:(f + 1) * PIECE], m_acc[f % 4][:, 0:PIECE], ACT.Copy).then_inc(mh_rdy, 1)

            def sign_fc(k):
                act.wait_ge(ld_fc, 16)
                link(act.activation(qfc[:, k, :], fc_raw[:, k, :], ACT.Sign))

            def abs_fc(k):
                act.activation(fc_raw[:, k, :], fc_raw[:, k, :], ACT.Abs, accum_out=part[:, 0, k:k + 1]).then_inc(abs_rdy, 1)

            def sign_abs_proj(c):
                act.wait_ge(ld_proj, 16)
                link(act.activation(qproj[:, c, :], proj_raw[:, c, :], ACT.Sign))
                act.activation(proj_raw[:, c, :], proj_raw[:, c, :], ACT.Abs,
                               accum_out=part[:, 1, c:c + 1]).then_inc(abs_rdy, 1)

            for f in range(NPC):
                act.wait_ge(fold_mm, f + 1)
                act.activation(mt[:, 2 * f:2 * f + 2, :],
                               fold_acc[f % 2][:, 0:2 * FWS].rearrange("p (c w) -> p c w", w=FWS)[:, :, 0:FW],
                               ACT.Copy).then_inc(mt_rdy, 1)
                if f >= 1:
                    m_hi(f - 1)
                if f == 4:
                    act.wait_ge(rb_mm, 1)
                    for i in range(2):
                        last = act.activation(r_b[:, 320 * i:320 * i + 320], rb_acc[i][:, 0:320], ACT.Copy)
                    last.then_inc(rb_rdy, 1)
                if f == 7:
                    act.wait_ge(lsum_rdy, 1)
                    act.activation(lame[:, :], lams[:, :], ACT.Exp).then_inc(lexp_rdy, 1)
                if f == 8:
                    sign_fc(0)

            def evacuate(u0, u1):
                for u in range(u0, u1):
                    if is_q(u):
                        _, half, c = uses[u]
                        g0, g1 = groups(half)
                        if half == 1 and c == 0:
                            act.wait_ge(zeros, 3)
                        act.wait_ge(ring_mm, u + 1)
                        for s in range(2):
                            r0 = GP * s
                            last = act.activation(
                                qbd[r0:r0 + GP, g0:g1, c, s, 0:GTOK],
                                ring[u % 3][r0:r0 + GP, 0:(g1 - g0) * GTOK].rearrange("p (g q) -> p g q", q=GTOK),
                                ACT.Identity, bias=mt[r0:r0 + GP, c, P:FW])
                        last.then_inc(q_ev, 1)

            act.wait_ge(zeros, 2)
            evacuate(0, 1)
            m_hi(NPC - 1)
            evacuate(1, n_first)

            def exps(g):
                act.wait_ge(d_rdy, g + 1)
                act.activation(e[g % 3][:, :, :], e[g % 3][:, :, :], ACT.Exp, scale=rq8[:, g:g + 1]).then_inc(e_rdy, 1)

            def scale_keys(T):
                act.wait_ge(at_mm, T + 1)
                if T >= 2:
                    act.wait_ge(av_mm, T - 1)
                act.activation(ats[T % 2][:, :, :, :], at_acc.rearrange("p (j h q) -> p j h q", h=2, q=GP),
                               ACT.Copy, scale=rk[:, T:T + 1]).then_inc(at_rdy, 1)

            def output(T):
                act.wait_ge(av_mm, T + 1)
                if T >= 2:
                    act.wait_ge(ms_rdy, T - 1)
                n_gp = len(gps(T))
                o_ = o_ps[:, 0:n_gp, 0:NHP * DH].rearrange("p g (j d) -> p g j d", d=DH)
                act.activation(osq[T % 2][:, 0:n_gp, :, :], o_, ACT.Square)
                act.activation(on[:, T, 0:n_gp, :, :], o_, ACT.Copy).then_inc(on_rdy, 1)

            def o_transposed(T):
                act.wait_ge(ot_mm, T + 1)
                for i in gps(T):
                    g = 2 * T + i
                    for j in range(2):
                        last = act.activation(
                            ot[:, 2 * j:2 * j + 2, g * GTOK:(g + 1) * GTOK],
                            ot_acc[T % 2][:, (2 * i + j) * P:(2 * i + j + 1) * P].rearrange(
                                "p (h q) -> p h q", q=GP)[:, :, 0:GTOK], ACT.Copy)
                last.then_inc(ot_rdy, 1)

            def rms_root(b):
                m = len(batch_groups(b))
                act.wait_ge(msq_rdy, b + 1)
                act.activation(nt[:, 1, 0:m], nx[:, min(b, 1), 0:m], ACT.Sqrt).then_inc(root_rdy, 1)

            def z_root(n, t0, t1):
                act.wait_ge(var_rdy, n)
                act.activation(lt[:, t0:t1], lx[:, t0:t1], ACT.Sqrt).then_inc(lroot_rdy, 1)

            def z_row(i):
                act.wait_ge(shift_rdy, 1 if i < FFN_TILES[0][1] else 2)
                if i >= 3:
                    act.wait_ge(zt_mm, i - 2)
                act.activation(z[i % 3][:, :], h[:, i, :], ACT.Identity, bias=lshift[:, i:i + 1],
                               scale=linv[:, i:i + 1]).then_inc(z_rdy, 1)

            def z_hi(i):
                act.wait_ge(zt_mm, i + 1)
                act.activation(zth[:, :, i * P:(i + 1) * P], zt_acc[i % 2].rearrange("p (k t) -> p k t", t=P),
                               ACT.Copy).then_inc(zth_rdy, 1)

            def g_hi(k):
                half, c = divmod(k, HC)
                t0, t1 = FFN_TILES[half]
                act.wait_ge(squ_rdy, k + 1)
                act.activation(gh[:, c, t0 * P:t1 * P], squ[k % 2][:, 0:(t1 - t0) * P], ACT.Copy).then_inc(gh_rdy, 1)

            for g in range(NG):
                if pair_of_step(g) is not None:
                    scale_keys(pair_of_step(g))
                exps(g)
                evacuate(fill[g], fill[g + 1])
                if pair_of_step(g) is not None:
                    output(pair_of_step(g))
                if g in (1, 3, 6):
                    sign_fc({1: 1, 3: 2, 6: 3}[g])
                if g in (0, 2, 5, 7):
                    abs_fc({0: 0, 2: 1, 5: 2, 7: 3}[g])
                if g == 8:
                    act.wait_ge(ring_mm, n_uses)
                if g >= 8:
                    sign_abs_proj(g - 8)
            scale_keys(4)
            rms_root(1)
            o_transposed(0)
            output(4)
            scale_keys(5)
            o_transposed(1)
            output(5)
            rms_root(2)
            sign_abs_proj(3)
            o_transposed(2)
            o_transposed(3)
            for c in range(4, 7):
                sign_abs_proj(c)
            o_transposed(4)
            o_transposed(5)
            z_root(1, 0, 2)
            z_row(0)
            z_row(1)
            sign_abs_proj(7)
            sign_abs_proj(8)
            z_hi(0)
            z_hi(1)
            sign_abs_proj(9)
            for k in range(2 * HC):
                half, c = divmod(k, HC)
                n_tok = (FFN_TILES[half][1] - FFN_TILES[half][0]) * P
                act.wait_ge(fc_mm, k + 1)
                if k >= 2:
                    act.wait_ge(squ_rdy, k - 1)
                act.activation(rel[k % 2][:, 0:n_tok], fc_acc[k % 2][:, 0:n_tok], ACT.Relu,
                               scale=H_SCALE / Z_SCALE).then_inc(rel_rdy, 1)
                if k >= 1 and k != HC:
                    g_hi(k - 1)
                if k == 1:
                    z_root(2, 2, TT)
                if k in (2, 3, 4):
                    z_row(k)
                if k in (5, 7, 9):
                    z_hi((k - 1) // 2)
                if k == HC - 1:
                    g_hi(k)
            g_hi(2 * HC - 1)

        @block.vector
        def _(dve):
            n = [0]

            def link(ins):
                n[0] += 1
                ins.then_inc(vchain, 1)
                dve.wait_ge(vchain, n[0])

            dve.wait_ge(mean_rdy, 1)
            dve.tensor_tensor(wc[:, :, :], wpos[:, :, :], mean_acc[:, 0:FW].unsqueeze(1).to_broadcast([P, KD, FW]),
                              ALU.subtract).then_inc(wc_rdy, 1)
            dve.wait_ge(ld_b, 16)
            for i in range(TT):
                dve.wait_ge(h_mm, i + 1)
                dve.tensor_tensor(h[:, i, :], h_acc[i], b_b[:, :], ALU.add).then_inc(h_ev, 1)
            for i in range(TT):
                dve.wait_ge(h_ev, i + 1)
                link(dve.bn_stats(bnst[:, i, :], h[:, i, :]))
                link(dve.bn_aggr(stat[:, i, :], bnst[:, i, :]))
            link(dve.tensor_scalar(lx[:, :], stat[:, :, 1], LN_EPS, None, ALU.add))
            link(rsqrt_guess(dve, link, ly[:, :], lx[:, :]))
            y = ly[:, :].bitcast(F32)
            for _ in range(3):
                link(dve.scalar_tensor_tensor(lt[:, :], y, -0.5, y, ALU.mult, ALU.mult))
                link(dve.tensor_tensor(lt[:, :], lt[:, :], lx[:, :], ALU.mult))
                link(dve.scalar_tensor_tensor(y, lt[:, :], 1.5, y, ALU.add, ALU.mult))
            dve.wait_ge(consts, 3)
            dve.tensor_tensor(diag[:, :, :], ident[:, :].unsqueeze(1).to_broadcast([P, TT, P]),
                              ly[:, :].bitcast(F32).unsqueeze(2).to_broadcast([P, TT, P]),
                              ALU.mult).then_inc(dg_rdy, 1)
            full = NG - 1
            rest = TOK - full * GTOK
            dve.wait_ge(ph_rdy, 1)
            dve.tensor_tensor(pl[:, 0:full, 0:GTOK], pt[:, 0:full * GTOK].rearrange("p (g q) -> p g q", q=GTOK),
                              ph[:, 0:full, 0:GTOK].bitcast(F32), ALU.subtract)
            dve.tensor_tensor(pl[:, full, 0:rest], pt[:, full * GTOK:], ph[:, full, 0:rest].bitcast(F32),
                              ALU.subtract).then_inc(pl_rdy, 1)
            dve.wait_ge(ld_lam, 16)
            link(dve.tensor_tensor(lamp[:, :, :], lamt[:, :, 0, :], lamt[:, :, 1, :], ALU.mult))
            dve.tensor_reduce(lams[:, :], lamp[:, :, :], AX.X, ALU.add).then_inc(lsum_rdy, 1)

            def m_lo(f):
                dve.wait_ge(mh_rdy, f + 1)
                dve.tensor_tensor(ml[:, f * PIECE:(f + 1) * PIECE], m_acc[f % 4][:, 0:PIECE],
                                  mh[:, f * PIECE:(f + 1) * PIECE].bitcast(F32), ALU.subtract).then_inc(ml_rdy, 1)

            for f in range(NPC - 1):
                m_lo(f)
                if f == 5:
                    dve.wait_ge(rb_rdy, 1)
                    dve.wait_ge(zeros, 1)
                    dve.wait_ge(consts, 6)
                    link(dve.tensor_tensor(rsel[:, :, :], r_b[:, :].rearrange("p (g q) -> p g q", q=GTOK),
                                           sel[:, :].unsqueeze(1).to_broadcast([P, NG, GTOK]), ALU.mult))
                    link(dve.tensor_reduce(rq[:, 0:NG], rsel[:, :, :], AX.X, ALU.add))
                    dve.tensor_scalar(rq8[:, :], rq[:, :], DH ** -0.5, None, ALU.mult)
                    pairs = rq[:, :].rearrange("p (t g) -> p t g", g=2)
                    for i in range(2):
                        last = dve.tensor_copy(rk[GP * i:GP * i + GP, :], pairs[GP * i:GP * i + GP, :, i])
                    last.then_inc(rk_rdy, 1)
            def evacuate(u0, u1):
                for u in range(u0, u1):
                    if is_q(u):
                        continue
                    kind, half, c = uses[u]
                    dve.wait_ge(ring_mm, u + 1)
                    if kind == "qk":
                        g0, g1 = groups(half)
                        t0, t1 = g0 * GTOK, g1 * GTOK
                        dve.scalar_tensor_tensor(kt[:, c - NPAIR, t0:t1], ring[u % 3][:, 0:t1 - t0], mt[:, c, P:FW],
                                                 r_b[:, t0:t1], ALU.add, ALU.mult).then_inc(kv_ev, 1)
                    else:
                        dve.tensor_tensor(v[:, half, :], ring[u % 3], cv_b[:, :], ALU.add).then_inc(kv_ev, 1)

            def threshold(k, total):
                dve.wait_ge(ab_mm, k + 1)
                link(dve.tensor_scalar(am[:, k:k + 1], total, 1.0 / (D * HID), 1e-5, ALU.mult, ALU.max))
                dve.tensor_scalar(thr[:, k:k + 1], am[:, k:k + 1], 0.7, None, ALU.mult).then_inc(thr_rdy, 1)
                dve.wait_ge(thr_rdy, k + 1)

            def ternary(q, w, k):
                return dve.scalar_tensor_tensor(q, w, thr[:, k:k + 1], q, ALU.is_gt, ALU.mult)

            def minus_max(g):
                s3 = s_acc[g % 2].rearrange("p (c k) -> p c k", k=GP)
                dve.wait_ge(s_mm, g + 1)
                link(dve.tensor_reduce(mx[:, g % 2, :], s3, AX.X, ALU.max))
                if g >= 3:
                    dve.wait_ge(a_rdy, g - 2)
                dve.tensor_tensor(e[g % 3][:, :, :], s3, mx[:, g % 2, :].unsqueeze(2).to_broadcast([P, NPAIR, GP]),
                                  ALU.subtract).then_inc(d_rdy, 1)

            def sums(g):
                dve.wait_ge(e_rdy, g + 1)
                link(dve.tensor_reduce(ssum[:, g % 2, :], e[g % 3][:, :, :], AX.X, ALU.add))
                link(dve.reciprocal(sinv[:, g, :], ssum[:, g % 2, :]))
                dve.scalar_tensor_tensor(ratio[:, g % 3, :], ssum[:, g % 2, 0:NHP], neglam[:, :],
                                         sinv[:, g, NHP:], ALU.mult, ALU.mult).then_inc(rat_rdy, 1)

            def sum_squares(T):
                n_gp = len(gps(T))
                dve.wait_ge(on_rdy, T + 1)
                dve.tensor_reduce(ms[:, 2 * T:2 * T + n_gp].rearrange("p g j c -> p (g j c)"),
                                  osq[T % 2][:, 0:n_gp].rearrange("p g j (c d) -> p (g j c) d", d=RMSW),
                                  AX.X, ALU.add).then_inc(ms_rdy, 1)

            def mean_squares(b):
                g0, m = batch_groups(b)[0], len(batch_groups(b))
                si = sinv[:, g0:g0 + m, 0:NHP]
                link(dve.scalar_tensor_tensor(sinv2[:, 0:m, :], si, 1.0 / RMSW / (1 - L_INIT) ** 2, si,
                                              ALU.mult, ALU.mult))
                dve.wait_ge(ms_rdy, BATCHES[b][1])
                s2 = sinv2[:, 0:m, :].rearrange("p g j -> p (g j)").unsqueeze(2).to_broadcast([P, NHP * m, RMSW])
                link(dve.tensor_tensor(nx[:, min(b, 1), 0:m].rearrange("p g j c -> p (g j) c"),
                                       ms[:, g0:g0 + m].rearrange("p g j c -> p (g j) c"), s2, ALU.mult))
                last = dve.tensor_scalar(nx[:, min(b, 1), 0:m], nx[:, min(b, 1), 0:m], RMS_EPS / (1 - L_INIT) ** 2, None, ALU.add)
                if b == 0:
                    link(last)
                    last = rsqrt_guess(dve, link, ny[:, b, 0:m], nx[:, min(b, 1), 0:m])
                last.then_inc(msq_rdy, 1)

            def rms_factors(b):
                g0, m = batch_groups(b)[0], len(batch_groups(b))
                dve.wait_ge(root_rdy, b)
                if b >= 2:
                    dve.wait_ge(on2_rdy, BATCHES[b - 2][1])
                f = ny[:, b % 2, 0:m].bitcast(F32)
                link(dve.reciprocal(f, nt[:, 1, 0:m]))
                dve.tensor_tensor(f, f,
                                  sinv[:, g0:g0 + m, 0:NHP].unsqueeze(3).to_broadcast([P, m, NHP, RMSW]),
                                  ALU.mult).then_inc(rms_rdy, 1)

            def z_lo(i):
                dve.wait_ge(zth_rdy, i + 1)
                dve.tensor_tensor(ztl[:, :, i * P:(i + 1) * P], zt_acc[i % 2].rearrange("p (k t) -> p k t", t=P),
                                  zth[:, :, i * P:(i + 1) * P], ALU.subtract).then_inc(ztl_rdy, 1)

            def residual(i):
                dve.wait_ge(wo_mm, i + 1)
                dve.tensor_tensor(h[:, i, :], h[:, i, :], wo_acc[i % 2], ALU.add).then_inc(h1_rdy, 1)
                dve.wait_ge(h1_rdy, i + 1)
                link(dve.bn_stats(bnst[:, i, :], h[:, i, :]))
                link(dve.bn_aggr(stat2[:, i, :], bnst[:, i, :]))

            def z_vars(t0, t1):
                dve.tensor_scalar(lx[:, t0:t1], stat2[:, t0:t1, 1], LN_EPS, Z_SCALE ** -2,
                                  ALU.add, ALU.mult).then_inc(var_rdy, 1)

            def z_factors(n, t0, t1):
                dve.wait_ge(lroot_rdy, n)
                link(dve.reciprocal(linv[:, t0:t1], lt[:, t0:t1]))
                dve.scalar_tensor_tensor(lshift[:, t0:t1], stat2[:, t0:t1, 0], -1.0, linv[:, t0:t1],
                                         ALU.mult, ALU.mult).then_inc(shift_rdy, 1)

            def ternary_fc(k):
                ternary(qfc[:, k, :], fc_raw[:, k, :], 0).then_inc(qfc_rdy, 1)

            def ternary_proj(c):
                ternary(qproj[:, c, :], proj_raw[:, c, :], 1).then_inc(qproj_rdy, 1)

            m_lo(NPC - 1)
            dve.wait_ge(mt_rdy, NPC)
            evacuate(0, 4)
            dve.tensor_tensor(diag[:, 0:KD, :], ident[:, :].unsqueeze(1).to_broadcast([P, KD, P]),
                              mt[:, 2 * NPAIR:, P].unsqueeze(2).to_broadcast([P, KD, P]), ALU.mult).then_inc(dv_rdy, 1)
            evacuate(4, 8)
            dve.wait_ge(cv_mm, 1)
            dve.tensor_copy(cv_b[:, :], cv_acc).then_inc(cv_rdy, 1)
            dve.wait_ge(cv_rdy, 1)
            evacuate(8, n_first)
            dve.wait_ge(lexp_rdy, 1)
            link(dve.scalar_tensor_tensor(neglam[:, :], lame[:, 1:2], L_INIT, lame[:, 0:1], ALU.subtract, ALU.subtract))
            for g in range(NG):
                if g == NG - 1:
                    sums(g - 1)
                minus_max(g)
                evacuate(fill[g], fill[g + 1])
                if g == 10:
                    threshold(0, abs_acc[0])
                if 1 <= g < NG - 1:
                    sums(g - 1)
                if g >= 5 and g % 2 == 1:
                    sum_squares((g - 5) // 2)
                if g == 8:
                    dve.wait_ge(abs_rdy, KD)
                    dve.tensor_reduce(psm[:, 0:1], part[:, 0, 0:KD], AX.X, ALU.add).then_inc(ab_rdy, 1)
                if g == 7:
                    mean_squares(0)
            sums(NG - 1)
            sum_squares(3)
            mean_squares(1)
            rms_factors(1)
            sum_squares(4)
            sum_squares(5)
            mean_squares(2)
            rms_factors(2)
            residual(0)
            ternary_fc(0)
            residual(1)
            z_vars(0, 2)
            ternary_fc(1)
            z_factors(1, 0, 2)
            ternary_fc(2)
            residual(2)
            ternary_fc(3)
            residual(3)
            z_lo(0)
            z_lo(1)
            residual(4)
            z_vars(2, TT)
            dve.wait_ge(abs_rdy, KD + HC)
            dve.tensor_reduce(psm[:, 1:2], part[:, 1, :], AX.X, ALU.add).then_inc(ab_rdy, 1)

            def g_lo(k):
                half, c = divmod(k, HC)
                t0, t1 = FFN_TILES[half]
                dve.wait_ge(gh_rdy, k + 1)
                dve.tensor_tensor(gl[:, c, t0 * P:t1 * P], squ[k % 2][:, 0:(t1 - t0) * P], gh[:, c, t0 * P:t1 * P],
                                  ALU.subtract).then_inc(gl_rdy, 1)

            for k in range(2 * HC):
                g_lo(k)
                if k == 0:
                    z_factors(2, 2, TT)
                    threshold(1, abs_acc[1])
                if k < HC:
                    ternary_proj(k)
                if k in (4, 6, 8):
                    z_lo(k // 2)
            link(dve.tensor_scalar(sout[:, :], am[:, 0:1], am[:, 0:1], am[:, 1:2], ALU.mult, ALU.mult))
            link(dve.tensor_scalar(sout[:, :], sout[:, :], H_SCALE ** -2, None, ALU.mult))
            for i in range(TT):
                dve.wait_ge(pj_mm, i + 1)
                if i >= 2:
                    dve.wait_ge(st_out[i % 2], 16 * (i // 2))
                dve.scalar_tensor_tensor(orow[i % 2][:, :], pj_acc[i % 2], sout[:, :], h[:, i, :],
                                         ALU.mult, ALU.add).then_inc(o_rdy, 1)

        @block.tensor
        def _(pe):
            def mm(o, l, r, start, stop):
                return pe.matmul(o, l, r, start=start, stop=stop, skip_group_check=True)

            pe.wait_ge(consts, 1)
            pe.wait_ge(ld_wpos, 16)
            for k in range(KD):
                last = mm(mean_acc[:, 0:FW], mean_w[:, :], wpos[:, k, :], k == 0, k == KD - 1)
            last.then_inc(mean_rdy, 1)
            pe.wait_ge(ld_x, 16)
            pe.wait_ge(ld_wcol, 16)
            for i in range(TT):
                mm(h_acc[i], pt[:, i * P:(i + 1) * P], wcol[:, :], True, True).then_inc(h_mm, 1)

            def transpose_piece(f):
                pe.wait_ge(mt_rdy, f + 1)
                if f >= 4:
                    pe.wait_ge(ml_rdy, f - 3)
                elif f == 0:
                    pe.wait_ge(h_ev, TT)
                for c in range(2):
                    last = pe.transpose(m_acc[f % 4][:, c * P:(c + 1) * P], mt[:, 2 * f + c, 0:P], ident[:, :])
                last.then_inc(tr_mm, 1)

            pe.wait_ge(wc_rdy, 1)
            pe.wait_ge(consts, 3)
            for f in range(NPC):
                pe.wait_ge(ld_qkv[f], 16)
                if f >= 2:
                    pe.wait_ge(mt_rdy, f - 1)
                for c in range(2):
                    for k in range(KD):
                        last = mm(fold_acc[f % 2][:, c * FWS:c * FWS + FW], wqkv_s[:, f, k, c * P:(c + 1) * P],
                                  wc[:, k, :], k == 0, k == KD - 1)
                last.then_inc(fold_mm, 1)
                if f >= 1:
                    transpose_piece(f - 1)
                if f == 4:
                    pe.wait_ge(dg_rdy, 1)
                    dg = diag[:, :, :].rearrange("p t q -> p (t q)")
                    for i in range(2):
                        last = mm(rb_acc[i][:, 0:320], ones[:, :], dg[:, 320 * i:320 * i + 320], True, True)
                    last.then_inc(rb_mm, 1)

            def project(u0, u1):
                for u in range(u0, u1):
                    kind, half, c = uses[u]
                    if u >= 3:
                        pe.wait_ge(*evacuated(u - 3))
                    if u < n_first:
                        pe.wait_ge(ml_rdy, c // 2 + 1 if kind == "qk" else NPC)
                    if kind == "qk":
                        g0, g1 = groups(half)
                        o = ring[u % 3][:, 0:(g1 - g0) * GTOK]
                        w = slice(c * P, (c + 1) * P)
                        mm(o, mh[:, w], ph[:, g0:g1, 0:GTOK], True, False)
                        mm(o, mh[:, w], pl[:, g0:g1, 0:GTOK], False, False)
                        last = mm(o, ml[:, w], ph[:, g0:g1, 0:GTOK], False, True)
                    else:
                        T = half
                        o = ring[u % 3]
                        xh = ph[:, 2 * T:2 * T + 2, :].rearrange("p g q -> p (g q)")
                        xl = pl[:, 2 * T:2 * T + 2, :].rearrange("p g q -> p (g q)")
                        mm(o, xh, mh[:, 4 * D:], True, False)
                        mm(o, xh, ml[:, 4 * D:], False, False)
                        last = mm(o, xl, mh[:, 4 * D:], False, True)
                    last.then_inc(ring_mm, 1)

            pe.wait_ge(zeros, 1)
            pe.wait_ge(pl_rdy, 1)
            pe.wait_ge(rb_rdy, 1)
            pe.wait_ge(ml_rdy, NPC - 2)
            project(0, 1)
            transpose_piece(NPC - 1)
            project(1, 6)
            pe.wait_ge(dv_rdy, 1)
            mm(cv_acc, ones[:, :], diag[:, 0:KD, :].rearrange("p t q -> p (t q)"), True, True).then_inc(cv_mm, 1)
            project(6, n_first)
            pe.wait_ge(consts, 7)
            pe.wait_ge(cv_rdy, 1)

            def scores(g):
                if g in (0, HALF_G[0]):
                    u = (n_first if g == 0 else n_second) - 1
                    nq = sum(is_q(w) for w in range(u + 1))
                    pe.wait_ge(q_ev, nq)
                    pe.wait_ge(kv_ev, u + 1 - nq)
                if g >= 2:
                    pe.wait_ge(d_rdy, g - 1)
                mm(s_acc[g % 2], ident_b[:, :], mask[:, :, :].rearrange("p c k -> p (c k)"), True, False)
                for c in range(NPAIR):
                    last = mm(s_acc[g % 2][:, c * GP:c * GP + GTOK],
                              qbd[:, g, c, :, :].rearrange("p h q -> p (h q)"),
                              kt[:, c, g * GTOK:(g + 1) * GTOK], False, c == NPAIR - 1)
                last.then_inc(s_mm, 1)

            def transpose_a(T):
                pe.wait_ge(a_rdy, min(2 * T + 2, NG))
                if T >= 1:
                    pe.wait_ge(at_rdy, T)
                for j in range(NHP):
                    last = pe.transpose(at_acc[:, j * P:(j + 1) * P],
                                        a[T % 2][:, j, :, :].rearrange("p g k -> p (g k)"), ident[:, :])
                last.then_inc(at_mm, 1)

            def apply(T):
                pe.wait_ge(at_rdy, T + 1)
                if T >= 3:
                    pe.wait_ge(*evacuated(n_second + T - 3))
                if T >= 1:
                    pe.wait_ge(on_rdy, T)
                for i in gps(T):
                    r0 = GP * i
                    for j in range(NHP):
                        for s in range(2):
                            last = mm(o_ps[GP * s:GP * s + GP, i, j * DH:(j + 1) * DH],
                                      ats[T % 2][r0:r0 + GTOK, j, s, :],
                                      v[r0:r0 + GTOK, T, (2 * j + s) * DH:(2 * j + s + 1) * DH], True, True)
                last.then_inc(av_mm, 1)

            def transpose_o(T):
                pe.wait_ge(on2_rdy, T + 1)
                if T >= 2:
                    pe.wait_ge(ot_rdy, T - 1)
                for i in gps(T):
                    for j in range(2):
                        last = pe.transpose(ot_acc[T % 2][:, (2 * i + j) * P:(2 * i + j + 1) * P],
                                            on[:, T, i, 2 * j:2 * j + 2, :].rearrange("p j d -> p (j d)"), ident[:, :])
                last.then_inc(ot_mm, 1)

            def transpose_z(i):
                pe.wait_ge(z_rdy, i + 1)
                if i == 1:
                    pe.wait_ge(ot_rdy, NT)
                if i >= 2:
                    pe.wait_ge(ztl_rdy, i - 1)
                for k in range(KD):
                    last = pe.transpose(zt_acc[i % 2][:, k * P:(k + 1) * P], z[i % 3][:, k * P:(k + 1) * P], ident[:, :])
                last.then_inc(zt_mm, 1)

            def project_out(i):
                t = slice(i * P, (i + 1) * P)
                pe.wait_ge(ot_rdy, min(NT, -(-(i + 1) * P // (2 * GTOK))))
                if i >= 2:
                    pe.wait_ge(h1_rdy, i - 1)
                for k in range(KD):
                    last = mm(wo_acc[i % 2], ot[:, k, t], wo_s[:, k, :], k == 0, k == KD - 1)
                last.then_inc(wo_mm, 1)

            for g in range(NG):
                if pair_of_step(g) is not None:
                    transpose_a(pair_of_step(g))
                scores(g)
                project(fill[g], fill[g + 1])
                if pair_of_step(g) is not None:
                    apply(pair_of_step(g))
                if g == 9:
                    pe.wait_ge(ab_rdy, 1)
                    mm(abs_acc[0], ones[:, :], psm[:, 0:1], True, True).then_inc(ab_mm, 1)
            transpose_a(4)
            pe.wait_ge(thr_rdy, 1)
            transpose_o(0)
            apply(4)
            transpose_a(5)
            transpose_o(1)
            apply(5)
            pe.wait_ge(ld_wo, 16)
            project_out(0)
            transpose_o(2)
            transpose_o(3)
            project_out(1)
            project_out(2)
            transpose_o(4)
            transpose_o(5)
            project_out(3)
            transpose_z(0)
            transpose_z(1)
            project_out(4)
            pe.wait_ge(qfc_rdy, KD)
            for half in range(2):
                t0, t1 = FFN_TILES[half]
                t = slice(t0 * P, t1 * P)
                pe.wait_ge(ztl_rdy, t1)
                for c in range(HC):
                    u = half * HC + c
                    if u >= 2:
                        pe.wait_ge(rel_rdy, u - 1)
                    for k in range(KD):
                        w = qfc[:, k, c * P:(c + 1) * P]
                        mm(fc_acc[u % 2][:, 0:(t1 - t0) * P], w, zth[:, k, t], k == 0, False)
                        last = mm(fc_acc[u % 2][:, 0:(t1 - t0) * P], w, ztl[:, k, t], False, k == KD - 1)
                    last.then_inc(fc_mm, 1)
                    if u == 1:
                        pe.wait_ge(ab_rdy, 2)
                        mm(abs_acc[1], ones[:, :], psm[:, 1:2], True, True).then_inc(ab_mm, 1)
                    if half == 0 and c in (4, 6, 8):
                        transpose_z(c // 2)
            pe.wait_ge(qproj_rdy, HC)
            pe.wait_ge(thr_rdy, 2)
            for i in range(TT):
                t = slice(i * P, (i + 1) * P)
                pe.wait_ge(gl_rdy, HC if i < FFN_TILES[0][1] else 2 * HC)
                if i >= 2:
                    pe.wait_ge(o_rdy, i - 1)
                for c in range(HC):
                    mm(pj_acc[i % 2], gh[:, c, t], qproj[:, c, :], c == 0, False)
                    last = mm(pj_acc[i % 2], gl[:, c, t], qproj[:, c, :], False, c == HC - 1)
                last.then_inc(pj_mm, 1)


def kernel(x, L0_tok_W, L0_tok_b, L0_attn_l_q1, L0_attn_l_k1, L0_attn_l_q2, L0_attn_l_k2, L0_attn_wq, L0_attn_wk,
           L0_attn_wv, L0_attn_wo, L0_ffn_w_fc, L0_ffn_w_proj):
    import concourse.bacc as bacc
    import numpy as np
    from concourse.bass_utils import run_bass_kernel_spmd

    f = np.ascontiguousarray
    xs = np.asarray(x)[:, :, 0]
    patches = np.stack([xs[:, STRIDE * n:STRIDE * n + P] for n in range(NPATCH)], axis=1)
    W, bias = np.asarray(L0_tok_W), np.asarray(L0_tok_b)
    wb = np.concatenate([W, bias[:, None]], axis=1)
    wqkv = np.concatenate([np.asarray(L0_attn_wq), np.asarray(L0_attn_wk), np.asarray(L0_attn_wv)])
    wo = np.asarray(L0_attn_wo)
    arrays = {
        "xT": f(patches.reshape(TOK, P).T),
        "w_pos": f(wb.reshape(KD, P, FW).transpose(1, 0, 2)),
        "w_col": f(W.T),
        "b": f(bias),
        "lam": f(np.stack([np.asarray(t) for t in (L0_attn_l_q1, L0_attn_l_k1, L0_attn_l_q2, L0_attn_l_k2)])
                 .reshape(2, 2, NH)),
        "wqkv": f(wqkv.reshape(NPC, PIECE, KD, P).transpose(0, 3, 2, 1)),
        "wo": f(wo.T.reshape(2, 2, 2, DH, D).transpose(1, 3, 0, 2, 4).reshape(P, KD, D)),
        "w_fc": f(np.asarray(L0_ffn_w_fc).reshape(HID, KD, P).transpose(2, 1, 0)),
        "w_proj": f(np.asarray(L0_ffn_w_proj).reshape(D, HC, P).transpose(2, 1, 0)),
    }
    nc = bacc.Bacc("TRN2", target_bir_lowering=False, num_devices=1)
    args = [nc.dram_tensor(n, t.shape, F32, kind="ExternalInput").ap() for n, t in arrays.items()]
    out = nc.dram_tensor("out", (TT, P, D), F32, kind="ExternalOutput").ap()
    audio_block(nc, *args, out)
    r = run_bass_kernel_spmd(nc, [arrays], core_ids=[0])
    return r.results[0]["out"].reshape(NB, NPATCH, D)
```

```python
import math
from contextlib import ExitStack

import concourse.bass as bass
from concourse import mybir

F32 = mybir.dt.float32
F32R = mybir.dt.float32r
F16 = mybir.dt.float16
BF16 = mybir.dt.bfloat16
I32 = mybir.dt.int32
ALU = mybir.AluOpType
ACT = mybir.ActivationFunctionType
AX = mybir.AxisListType

P = 128
NB, NPATCH, STRIDE = 64, 10, 64
D, NH, DH = 512, 8, 64
HID = 1280
KD = D // P
HC = HID // P
TOK = NB * NPATCH
TT = TOK // P
GTOK = 6 * NPATCH
GP = 64
NG = -(-TOK // GTOK)
NT = -(-NG // 2)
TOKG = NG * GTOK
NPAIR = 2 * NH // 2
NHP = NH // 2
QKV = 5 * D
PIECE = 256
NPC = QKV // PIECE
FW = P + 1
FWS = 132
L_INIT = 0.8 - 0.6 * math.exp(-0.3 * 1)
LN_EPS, RMS_EPS = 1e-5, 1e-6
RMSW = 8
BATCHES = ((0, 3), (3, 6))
BATCH_G = 6
MASKED = -1.0e30
Z_SCALE = 2.0 ** 11
H_SCALE = 2.0 ** -2
HALF_G = (6, NG - 6)
FFN_TILES = ((0, 3), (3, TT))
OUT_PIECES = [(i, 0, D) for i in range(TT - 1)] + [(TT - 1, 0, D // 2), (TT - 1, D // 2, D)]
LN_TILES = ((0, 2), (2, 3), (3, TT))
QK_ORDER = [c for j in range(NPAIR) for c in (j, NPAIR + j)]


def rsqrt_guess(dve, link, y, x):
    link(dve.tensor_scalar(y, x.bitcast(I32), 1, None, ALU.logical_shift_right))
    return dve.tensor_scalar(y, y, -1.0, float(0x5F3759DF), ALU.mult, ALU.add)


def audio_block(nc, xT, w_pos, w_col, b, lam, wqkv, wo, w_fc, w_proj, out):
    with ExitStack() as ctx:
        def at(name, shape, dtype, offset):
            return nc.alloc_sbuf_tensor_at(name, shape, dtype, offset=offset)

        def sem(name):
            return ctx.enter_context(nc.semaphore(name))

        top = [(nc.sbuf_base + 31) // 32 * 32]

        def region(size):
            start = top[0]
            top[0] += (size + 31) // 32 * 32
            return start

        ones = at("ones", [P, P], F32, region(512))
        mean_w = at("mean_w", [P, P], F32, region(512))
        ident = at("ident", [P, P], F32, region(512))
        ident_b = at("ident_b", [P, P], BF16, region(256))
        mask = at("mask", [P, NPAIR, GP], BF16, region(1024))
        cv_b = at("cv_b", [P, D], F32, region(2048))
        r_b = at("r_b", [P, TOKG], F32, region(4 * TOKG))
        rp = region(6144)
        ph = at("ph", [P, 2 * NT, GP], F32R, rp)
        pl = at("pl", [P, 2 * NT, GP], F32R, rp + 3072)
        h = at("h", [P, TT, D], F32, region(4 * TT * D))
        sel = at("sel", [P, GTOK], F32, region(4 * GTOK))
        lamt = at("lamt", [P, 2, 2, NH], F32, region(128))
        lamp = at("lamp", [P, 2, NH], F32, region(64))
        lams = at("lams", [P, 2], F32, region(8))
        lame = at("lame", [P, 2], F32, region(8))
        neglam = at("neglam", [P, 1], F32, region(4))
        bnst = at("bnst", [P, TT, 6], F32, region(120))
        stat = at("stat", [P, TT, 2], F32, region(40))
        stat2 = at("stat2", [P, TT, 2], F32, region(40))
        rtok = at("rtok", [P, TT], F32, region(20))
        rtok2 = at("rtok2", [P, TT], F32, region(20))
        rq = at("rq", [P, 2 * NT], F32, region(48))
        rq8 = at("rq8", [P, 2 * NT], F32, region(48))
        rk = at("rk", [P, NT], F32, region(24))
        nx = at("nx", [P, 2, BATCH_G, NHP, RMSW], F32, region(1536))
        nt = at("nt", [P, 2, BATCH_G, NHP, RMSW], F32, region(1536))
        ny = at("ny", [P, 2, BATCH_G, NHP, RMSW], F32, region(1536))
        linv = at("linv", [P, TT], F32, region(20))
        lshift = at("lshift", [P, TT], F32, region(20))
        lx = at("lx", [P, TT], F32, region(20))
        lt = at("lt", [P, TT], F32, region(20))
        ly = at("ly", [P, TT], I32, region(20))
        mx = at("mx", [P, 2, NPAIR], F32, region(64))
        ssum = at("ssum", [P, 2, NPAIR], F32, region(64))
        sinv = at("sinv", [P, NG, NPAIR], F32, region(4 * NG * NPAIR))
        sinv2 = at("sinv2", [P, BATCH_G, NHP], F32, region(96))
        ratio = at("ratio", [P, 3, NHP], F32, region(48))
        ms = at("ms", [P, 2 * NT, NHP, RMSW], F32, region(1536))
        part = at("part", [P, 2, HC], F32, region(80))
        psm = at("psm", [P, 2], F32, region(8))
        am = at("am", [P, 2], F32, region(8))
        thr = at("thr", [P, 2], F32, region(8))
        sout = at("sout", [P, 1], F32, region(4))

        ra = region(4 * KD * QKV)
        wqkv_s = at("wqkv_s", [P, NPC, KD, PIECE], F32, ra)
        fc_raw = at("fc_raw", [P, KD, HID], F32, ra)
        proj_raw = at("proj_raw", [P, HC, D], F32, ra + 4 * KD * HID)

        ffn_tile = 4 * max(t1 - t0 for t0, t1 in FFN_TILES) * P
        rqd = region(35840 + 4 * ffn_tile)
        qt = at("qt", [P, NPAIR, TOKG], F32, rqd)
        zth = at("zth", [P, KD, TOK], F16, rqd)
        ztl = at("ztl", [P, KD, TOK], F16, rqd + 5120)
        otl = at("otl", [P, NHP, TOKG], F32R, rqd + 10240)
        gh = at("gh", [P, HC, TOK], F16, rqd + 10240)
        gl = at("gl", [P, HC, TOK], F16, rqd + 23040)
        rel = [at(f"rel{i}", [P, 384], F32, rqd + 35840 + 1536 * i) for i in range(2)]
        squ = [at(f"squ{i}", [P, 384], F32, rqd + 38912 + 1536 * i) for i in range(2)]

        rkt = region(4 * NPAIR * TOKG)
        kt = at("kt", [P, NPAIR, TOKG], F32, rkt)
        z = [at(f"z{i}", [P, D], F32, rkt + 2048 * i) for i in range(3)]
        orow = [at(f"orow{i}", [P, D], F32, rkt + 6144 + 2048 * i) for i in range(2)]

        rv = region(4 * NT * D)
        v = at("v", [P, NT, D], F32, rv)
        on = at("on", [P, NT, 2, NHP, DH], F32, rv)

        rm = region(4 * (QKV // P) * FW)
        mt = at("mt", [P, QKV // P, FW], F32, rm)
        wo_s = at("wo_s", [P, KD, D], F32, rm)
        wo_l = at("wo_l", [P, KD, D], F32R, rm)
        wo_h = [at(f"wo_h{k}", [P, D], F32R, rp + 2048 * k if k < 3 else rm + 4 * KD * D) for k in range(KD)]

        rmm = region(max(8 * QKV, 4 * NHP * TOKG + 2 * HC * D))
        mh = at("mh", [P, QKV], F32R, rmm)
        ml = at("ml", [P, QKV], F32R, rmm + 4 * QKV)
        ot = at("ot", [P, NHP, TOKG], F32R, rmm)
        qproj = at("qproj", [P, HC, D], F16, rmm + 4 * NHP * TOKG)

        qfc = at("qfc", [P, KD, HID], F16, region(2 * KD * HID))

        rw = region(18432)
        pt = at("pt", [P, TOK], F32, rw)
        wcol = at("wcol", [P, D], F32, rw + 2560)
        wpos = at("wpos", [P, KD, FW], F32, rw + 4608)
        wc = at("wc", [P, KD, FW], F32, rw + 6688)
        b_b = at("b_b", [P, D], F32, rw + 8768)
        diag = at("diag", [P, TT, P], F32, rw + 10816)
        rsel = at("rsel", [P, NG, GTOK], F32, rw + 10816 + 2560)
        e = [at(f"e{i}", [P, NPAIR, GP], F32, rw + 2048 * i) for i in range(3)]
        a = [at(f"a{i}", [P, NHP, 2, GP], F32, rw + 6144 + 2048 * i) for i in range(2)]
        ats = [at(f"ats{i}", [P, NHP, 2, GP], F32, rw + 10240 + 2048 * i) for i in range(2)]
        osq = [at(f"osq{i}", [P, 2, NHP, DH], F32, rw + 14336 + 2048 * i) for i in range(2)]
        assert top[0] <= nc.sbuf_usable_end, (top[0], nc.sbuf_usable_end)

        bank = [ctx.enter_context(nc.psum_tensor(f"bank{i}", [P, 512], F32)) for i in range(3)]
        o_ps = ctx.enter_context(nc.psum_tensor("o_ps", [P, 2, 512], F32))
        bank += [o_ps[:, 0, :], o_ps[:, 1, :]]
        bank += [ctx.enter_context(nc.psum_tensor(f"bank{i}", [P, 512], F32)) for i in range(5, 8)]
        bank = [x[:, :] for x in bank]
        h_acc = (bank[0], bank[5], bank[7], bank[3], bank[4])
        fold_acc = (bank[1], bank[2])
        m_acc = (bank[3], bank[4], bank[0], bank[5])
        rb_acc = (bank[6], bank[7])
        cv_acc = bank[0]
        mean_acc = bank[6]
        ring = bank[5:8]
        s_acc = bank[0:2]
        at_acc = (bank[2], bank[2], bank[2], bank[6], bank[2], bank[6])
        wo_acc = bank[5:7]
        ot_acc = (bank[7], bank[1])
        zt_acc = (bank[2], bank[7])
        fc_acc = bank[0:2]
        pj_acc = (bank[3], bank[4])
        abs_acc = (bank[7][:, 0:1], bank[3][:, 0:1])

        ld_x, ld_wpos, ld_wcol = sem("ld_x"), sem("ld_wpos"), sem("ld_wcol")
        ld_lam, ld_b, ld_wo = sem("ld_lam"), sem("ld_b"), sem("ld_wo")
        ld_qkv = [sem(f"ld_qkv{f}") for f in range(NPC)]
        ld_fc, ld_proj = sem("ld_fc"), sem("ld_proj")
        st_out = [sem(f"st_out{i}") for i in range(2)]
        consts = sem("consts")
        pchain = sem("pchain")
        zeros = sem("zeros")
        ph_rdy, pl_rdy = sem("ph_rdy"), sem("pl_rdy")
        mean_rdy, wc_rdy = sem("mean_rdy"), sem("wc_rdy")
        h_mm, h_ev = sem("h_mm"), sem("h_ev")
        fold_mm, mt_rdy = sem("fold_mm"), sem("mt_rdy")
        tr_mm, mh_rdy, ml_rdy = sem("tr_mm"), sem("mh_rdy"), sem("ml_rdy")
        dg_rdy, rb_mm, rb_rdy, rk_rdy = sem("dg_rdy"), sem("rb_mm"), sem("rb_rdy"), sem("rk_rdy")
        dv_rdy, cv_mm, cv_rdy = sem("dv_rdy"), sem("cv_mm"), sem("cv_rdy")
        ring_mm = sem("ring_mm")
        q_ev = sem("q_ev")
        kv_ev = sem("kv_ev")
        s_mm, d_rdy, e_rdy, rat_rdy, a_rdy = sem("s_mm"), sem("d_rdy"), sem("e_rdy"), sem("rat_rdy"), sem("a_rdy")
        at_mm, at_rdy, av_mm, on_rdy = sem("at_mm"), sem("at_rdy"), sem("av_mm"), sem("on_rdy")
        ms_rdy, msq_rdy, root_rdy, rms_rdy, on2_rdy = (sem("ms_rdy"), sem("msq_rdy"), sem("root_rdy"), sem("rms_rdy"),
                                                       sem("on2_rdy"))
        woh_rdy, wol_rdy, wol_dve_rdy = sem("woh_rdy"), sem("wol_rdy"), sem("wol_dve_rdy")
        otl_rdy = sem("otl_rdy")
        ot_mm, ot_rdy, zt_mm, zth_rdy, ztl_rdy = (sem("ot_mm"), sem("ot_rdy"), sem("zt_mm"), sem("zth_rdy"),
                                                  sem("ztl_rdy"))
        var_rdy, lroot_rdy, shift_rdy = sem("var_rdy"), sem("lroot_rdy"), sem("shift_rdy")
        lsum_rdy, lexp_rdy = sem("lsum_rdy"), sem("lexp_rdy")
        abs_rdy, ab_rdy, ab_mm = sem("abs_rdy"), sem("ab_rdy"), sem("ab_mm")
        thr_rdy = sem("thr_rdy")
        qfc_rdy, qfc_pool_rdy, qproj_rdy = sem("qfc_rdy"), sem("qfc_pool_rdy"), sem("qproj_rdy")
        wo_mm, h1_rdy, z_rdy = sem("wo_mm"), sem("h1_rdy"), sem("z_rdy")
        fc_mm, rel_rdy, squ_rdy, gh_rdy, gl_rdy = (sem("fc_mm"), sem("rel_rdy"), sem("squ_rdy"), sem("gh_rdy"),
                                                   sem("gl_rdy"))
        pj_mm, o_rdy = sem("pj_mm"), sem("o_rdy")
        vchain = sem("vchain")
        achain = sem("achain")

        uses = [("qk", 0, c) for c in QK_ORDER] + [("v", T, 0) for T in range(3)]
        n_first = len(uses)
        uses += [("qk", 1, c) for c in QK_ORDER] + [("v", T, 0) for T in range(3, NT)]
        n_uses = len(uses)
        n_second = n_uses - (NT - 3)
        fill = [n_first + (n_second - n_first) * i // HALF_G[0] for i in range(HALF_G[0] + 1)]
        fill += range(n_second + 1, n_uses + 1)
        fill += [n_uses] * (NG + 1 - len(fill))

        def is_q(u):
            return uses[u][0] == "qk" and uses[u][2] < NPAIR

        def evacuated(u):
            n = sum(is_q(w) for w in range(u + 1))
            return (q_ev, n) if is_q(u) else (kv_ev, u + 1 - n)

        def groups(half):
            return (0, HALF_G[0]) if half == 0 else (HALF_G[0], NG)

        def gps(T):
            return range(min(2, NG - 2 * T))

        def batch_groups(b):
            return range(2 * BATCHES[b][0], min(2 * BATCHES[b][1], NG))

        block = ctx.enter_context(nc.Block())

        @block.sync
        def _(sp):
            sp.dma_start(wpos[:, :, :], w_pos).then_inc(ld_wpos, 16)
            sp.dma_start(pt[:, :], xT).then_inc(ld_x, 16)
            sp.dma_start(wcol[:, :], w_col).then_inc(ld_wcol, 16)
            sp.dma_start(wqkv_s[:, 0, :, :], wqkv[0]).then_inc(ld_qkv[0], 16)
            sp.dma_start(b_b[:, :], b.partition_broadcast(P)).then_inc(ld_b, 16)
            for f in range(1, NPC):
                sp.dma_start(wqkv_s[:, f, :, :], wqkv[f]).then_inc(ld_qkv[f], 16)
            sp.dma_start(lamt[:, :, :, :], lam.partition_broadcast(P)).then_inc(ld_lam, 16)
            sp.wait_ge(fold_mm, NPC // 2)
            sp.dma_start(fc_raw[:, :, :], w_fc).then_inc(ld_fc, 16)
            sp.wait_ge(fold_mm, NPC)
            sp.dma_start(proj_raw[:, :, :], w_proj).then_inc(ld_proj, 16)
            sp.wait_ge(q_ev, 2 * NPAIR)
            sp.wait_ge(*evacuated(n_second - 1))
            sp.dma_start(wo_s[:, :, :], wo).then_inc(ld_wo, 16)
            for n, (i, d0, d1) in enumerate(OUT_PIECES):
                sp.wait_ge(o_rdy, n + 1)
                sp.dma_start(out[i][:, d0:d1], orow[n % 2][:, 0:d1 - d0]).then_inc(st_out[n % 2], 16)
            for n in range(2):
                sp.wait_ge(st_out[n], 16 * len(range(n, len(OUT_PIECES), 2)))

        @block.gpsimd
        def _(pool):
            n = [0]

            def link(ins):
                n[0] += 1
                ins.then_inc(pchain, 1)
                pool.wait_ge(pchain, n[0])

            pool.memset(mean_w[:, :], 1.0 / D).then_inc(consts, 1)
            pool.memset(ones[:, :], 1.0).then_inc(consts, 1)
            link(pool.memset(ident[:, :], 0.0))
            pool.affine_select(out=ident[:, :], in_=ident[:, :], compare_op=ALU.not_equal, fill=1.0, base=0,
                               pattern=[[-1, P]], channel_multiplier=1).then_inc(consts, 1)
            for t in (ph, pl):
                pool.memset(t[:, :, GTOK:].bitcast(F32), 0.0)
                pool.memset(t[:, NG - 1, TOK - (NG - 1) * GTOK:GTOK].bitcast(F32), 0.0)
                pool.memset(t[:, NG, 0:GTOK].bitcast(F32), 0.0)
            pool.memset(rq[:, NG:], 0.0)
            pool.memset(r_b[:, TOK:], 0.0).then_inc(zeros, 1)
            pool.wait_ge(consts, 3)
            pool.wait_ge(zeros, 1)
            pool.tensor_copy(ident_b[:, :], ident[:, :]).then_inc(consts, 1)
            for half in range(2):
                s = GP * half
                pool.wait_ge(consts, 4 + half)
                pool.tensor_copy(sel[s:s + GP, :], ident[s:s + GP, s:s + GTOK]).then_inc(consts, 1)
            pool.wait_ge(consts, 6)
            link(pool.memset(mask[:, :, 0:GTOK], 0.0))
            link(pool.memset(mask[:, :, GTOK:], MASKED))
            for half in range(2):
                s = GP * half
                m = mask[s:s + GP, :, 0:GTOK]
                link(pool.affine_select(out=m, in_=m, compare_op=ALU.is_ge, fill=MASKED, base=NPATCH - 1,
                                        pattern=[[0, NPAIR], [NPATCH, 6], [0, NPATCH]], channel_multiplier=-1))
                last = pool.affine_select(out=m, in_=m, compare_op=ALU.is_ge, fill=MASKED, base=0,
                                          pattern=[[0, NPAIR], [-1, GTOK]], channel_multiplier=1)
                if half == 0:
                    link(last)
            last.then_inc(consts, 1)
            pool.wait_ge(consts, 7)
            def combine(g):
                T, i = divmod(g, 2)
                eg, ag = e[g % 3], a[T % 2]
                if T >= 2 and i == 0:
                    pool.wait_ge(at_mm, T - 1)
                pool.wait_ge(rat_rdy, g + 1)
                link(pool.tensor_tensor(eg[:, NHP:, :], eg[:, NHP:, :],
                                        ratio[:, g % 3, :].unsqueeze(2).to_broadcast([P, NHP, GP]), ALU.mult))
                pool.tensor_tensor(ag[:, :, i, :], eg[:, NHP:, :], eg[:, 0:NHP, :], ALU.add).then_inc(a_rdy, 1)

            def normalize(T):
                n_gp = len(gps(T))
                w = on[:, T, 0:n_gp].rearrange("p g j (c d) -> p (g j c) d", d=RMSW)
                g0 = 2 * T % BATCH_G
                y = ny[:, 2 * T // BATCH_G, g0:g0 + n_gp].rearrange("p g j c -> p (g j c)")
                pool.tensor_tensor(w, w, y.unsqueeze(2).to_broadcast([P, 32 * n_gp, RMSW]),
                                   ALU.mult).then_inc(on2_rdy, 1)

            def wo_lo(k):
                pool.wait_ge(woh_rdy, k + 1)
                pool.tensor_tensor(wo_l[:, k, :], wo_s[:, k, :], wo_h[k][:, :].bitcast(F32),
                                   ALU.subtract).then_inc(wol_rdy, 1)

            for g in range(NG):
                combine(g)
                if g == 7:
                    wo_lo(0)
            pool.wait_ge(thr_rdy, 1)
            for b in range(2):
                pool.wait_ge(rms_rdy, b + 1)
                for T in range(*BATCHES[b]):
                    normalize(T)
            for k in range(2, KD):
                link(pool.tensor_scalar(fc_raw[:, k, :], fc_raw[:, k, :], thr[:, 0:1], None, ALU.is_gt))
                pool.tensor_tensor(qfc[:, k, :], fc_raw[:, k, :], qfc[:, k, :], ALU.mult).then_inc(qfc_pool_rdy, 1)
            for k in range(2 * HC):
                n_tok = P * (FFN_TILES[k // HC][1] - FFN_TILES[k // HC][0])
                pool.wait_ge(rel_rdy, k + 1)
                if k >= 2:
                    pool.wait_ge(gl_rdy, k - 1)
                r_ = rel[k % 2][:, 0:n_tok]
                pool.tensor_tensor(squ[k % 2][:, 0:n_tok], r_, r_, ALU.mult).then_inc(squ_rdy, 1)

        @block.scalar
        def _(act):
            n = [0]

            def link(ins):
                n[0] += 1
                ins.then_inc(achain, 1)
                act.wait_ge(achain, n[0])

            full = (NG - 1)
            rest = TOK - full * GTOK
            act.wait_ge(ld_x, 16)
            act.activation(ph[:, 0:full, 0:GTOK], pt[:, 0:full * GTOK].rearrange("p (g q) -> p g q", q=GTOK), ACT.Copy)
            act.activation(ph[:, full, 0:rest], pt[:, full * GTOK:], ACT.Copy).then_inc(ph_rdy, 1)

            def m_hi(f):
                act.wait_ge(tr_mm, f + 1)
                act.activation(mh[:, f * PIECE:(f + 1) * PIECE], m_acc[f % 4][:, 0:PIECE], ACT.Copy).then_inc(mh_rdy, 1)

            def sign_fc(k):
                act.wait_ge(ld_fc, 16)
                link(act.activation(qfc[:, k, :], fc_raw[:, k, :], ACT.Sign))

            def abs_fc(k):
                act.activation(fc_raw[:, k, :], fc_raw[:, k, :], ACT.Abs, accum_out=part[:, 0, k:k + 1]).then_inc(abs_rdy, 1)

            def sign_abs_proj(c):
                act.wait_ge(ld_proj, 16)
                link(act.activation(qproj[:, c, :], proj_raw[:, c, :], ACT.Sign))
                act.activation(proj_raw[:, c, :], proj_raw[:, c, :], ACT.Abs,
                               accum_out=part[:, 1, c:c + 1]).then_inc(abs_rdy, 1)

            for f in range(NPC):
                act.wait_ge(fold_mm, f + 1)
                act.activation(mt[:, 2 * f:2 * f + 2, :],
                               fold_acc[f % 2][:, 0:2 * FWS].rearrange("p (c w) -> p c w", w=FWS)[:, :, 0:FW],
                               ACT.Copy).then_inc(mt_rdy, 1)
                if f >= 1:
                    m_hi(f - 1)
                if f == 4:
                    act.wait_ge(rb_mm, 1)
                    for i in range(2):
                        last = act.activation(r_b[:, 320 * i:320 * i + 320], rb_acc[i][:, 0:320], ACT.Copy)
                    last.then_inc(rb_rdy, 1)
                if f == 7:
                    act.wait_ge(lsum_rdy, 1)
                    act.activation(lame[:, :], lams[:, :], ACT.Exp).then_inc(lexp_rdy, 1)
                if f == 8:
                    sign_fc(0)

            def evacuate(u0, u1):
                for u in range(u0, u1):
                    if is_q(u):
                        _, half, c = uses[u]
                        g0, g1 = groups(half)
                        act.wait_ge(ring_mm, u + 1)
                        act.activation(qt[:, c, g0 * GTOK:g1 * GTOK], ring[u % 3][:, 0:(g1 - g0) * GTOK],
                                       ACT.Identity, bias=mt[:, c, P:FW]).then_inc(q_ev, 1)

            evacuate(0, 3)
            m_hi(NPC - 1)
            evacuate(3, n_first)

            def exps(g):
                act.wait_ge(d_rdy, g + 1)
                act.activation(e[g % 3][:, :, :], e[g % 3][:, :, :], ACT.Exp, scale=rq8[:, g:g + 1]).then_inc(e_rdy, 1)

            def scale_keys(T):
                act.wait_ge(at_mm, T + 1)
                if T >= 2:
                    act.wait_ge(av_mm, T - 1)
                act.activation(ats[T % 2][:, :, :, :], at_acc[T].rearrange("p (j h q) -> p j h q", h=2, q=GP),
                               ACT.Copy, scale=rk[:, T:T + 1]).then_inc(at_rdy, 1)

            def output(T):
                act.wait_ge(av_mm, T + 1)
                if T >= 2:
                    act.wait_ge(ms_rdy, T - 1)
                n_gp = len(gps(T))
                o_ = o_ps[:, 0:n_gp, 0:NHP * DH].rearrange("p g (j d) -> p g j d", d=DH)
                act.activation(osq[T % 2][:, 0:n_gp, :, :], o_, ACT.Square)
                act.activation(on[:, T, 0:n_gp, :, :], o_, ACT.Copy).then_inc(on_rdy, 1)

            def wo_hi(k):
                act.wait_ge(ld_wo, 16)
                act.activation(wo_h[k][:, :], wo_s[:, k, :], ACT.Copy).then_inc(woh_rdy, 1)

            def o_transposed(T):
                act.wait_ge(ot_mm, T + 1)
                for i in gps(T):
                    g = 2 * T + i
                    for j in range(2):
                        last = act.activation(
                            ot[:, 2 * j:2 * j + 2, g * GTOK:(g + 1) * GTOK],
                            ot_acc[T % 2][:, (2 * i + j) * P:(2 * i + j + 1) * P].rearrange(
                                "p (h q) -> p h q", q=GP)[:, :, 0:GTOK], ACT.Copy)
                last.then_inc(ot_rdy, 1)

            def rms_root(b):
                m = len(batch_groups(b))
                act.wait_ge(msq_rdy, b + 1)
                act.activation(nt[:, b, 0:m], nx[:, b, 0:m], ACT.Sqrt).then_inc(root_rdy, 1)

            def z_root(n):
                t0, t1 = LN_TILES[n]
                act.wait_ge(var_rdy, n + 1)
                act.activation(lt[:, t0:t1], lx[:, t0:t1], ACT.Sqrt).then_inc(lroot_rdy, 1)

            def z_row(i):
                act.wait_ge(shift_rdy, 1 + [t0 <= i < t1 for t0, t1 in LN_TILES].index(True))
                if i >= 3:
                    act.wait_ge(zt_mm, i - 2)
                act.activation(z[i % 3][:, :], h[:, i, :], ACT.Identity, bias=lshift[:, i:i + 1],
                               scale=linv[:, i:i + 1]).then_inc(z_rdy, 1)

            def z_hi(i):
                act.wait_ge(zt_mm, i + 1)
                act.activation(zth[:, :, i * P:(i + 1) * P], zt_acc[i % 2].rearrange("p (k t) -> p k t", t=P),
                               ACT.Copy).then_inc(zth_rdy, 1)

            def g_hi(k):
                half, c = divmod(k, HC)
                t0, t1 = FFN_TILES[half]
                act.wait_ge(squ_rdy, k + 1)
                act.activation(gh[:, c, t0 * P:t1 * P], squ[k % 2][:, 0:(t1 - t0) * P], ACT.Copy).then_inc(gh_rdy, 1)

            for g in range(NG):
                if g == NG - 1:
                    scale_keys(3)
                    wo_hi(2)
                    wo_hi(3)
                exps(g)
                if g in (4, 6, 8):
                    scale_keys((g - 4) // 2)
                evacuate(fill[g], fill[g + 1])
                if g >= 5 and g % 2 == 1:
                    output((g - 5) // 2)
                if g in (1, 3, 6):
                    sign_fc({1: 1, 3: 2, 6: 3}[g])
                if g in (0, 2, 5, 7):
                    abs_fc({0: 0, 2: 1, 5: 2, 7: 3}[g])
                if g == 8:
                    act.wait_ge(ring_mm, n_uses)
                    wo_hi(0)
                    wo_hi(1)
            output(3)
            scale_keys(4)
            rms_root(0)
            output(4)
            scale_keys(5)
            sign_abs_proj(0)
            output(5)
            o_transposed(0)
            o_transposed(1)
            rms_root(1)
            o_transposed(2)
            for c in range(1, 4):
                sign_abs_proj(c)
            o_transposed(3)
            sign_abs_proj(4)
            o_transposed(4)
            o_transposed(5)
            sign_abs_proj(5)
            sign_abs_proj(6)
            z_root(0)
            z_row(0)
            z_row(1)
            z_root(1)
            z_hi(0)
            z_hi(1)
            z_row(2)
            sign_abs_proj(7)
            z_hi(2)
            sign_abs_proj(8)
            for k in range(2 * HC):
                half, c = divmod(k, HC)
                n_tok = (FFN_TILES[half][1] - FFN_TILES[half][0]) * P
                act.wait_ge(fc_mm, k + 1)
                if k >= 2:
                    act.wait_ge(squ_rdy, k - 1)
                act.activation(rel[k % 2][:, 0:n_tok], fc_acc[k % 2][:, 0:n_tok], ACT.Relu,
                               scale=H_SCALE / Z_SCALE).then_inc(rel_rdy, 1)
                if k >= 1 and k != HC:
                    g_hi(k - 1)
                if k == 0:
                    sign_abs_proj(9)
                if k == 1:
                    z_root(2)
                if k in (2, 3):
                    z_row(k + 1)
                if k in (5, 7):
                    z_hi((k + 1) // 2)
                if k == HC - 1:
                    g_hi(k)
            g_hi(2 * HC - 1)

        @block.vector
        def _(dve):
            n = [0]

            def link(ins):
                n[0] += 1
                ins.then_inc(vchain, 1)
                dve.wait_ge(vchain, n[0])

            dve.wait_ge(mean_rdy, 1)
            dve.tensor_tensor(wc[:, :, :], wpos[:, :, :], mean_acc[:, 0:FW].unsqueeze(1).to_broadcast([P, KD, FW]),
                              ALU.subtract).then_inc(wc_rdy, 1)
            dve.wait_ge(ld_b, 16)
            for i in range(TT):
                dve.wait_ge(h_mm, i + 1)
                dve.tensor_tensor(h[:, i, :], h_acc[i], b_b[:, :], ALU.add).then_inc(h_ev, 1)
            for i in range(TT):
                dve.wait_ge(h_ev, i + 1)
                link(dve.bn_stats(bnst[:, i, :], h[:, i, :]))
                link(dve.bn_aggr(stat[:, i, :], bnst[:, i, :]))
            link(dve.tensor_scalar(lx[:, :], stat[:, :, 1], LN_EPS, None, ALU.add))
            link(rsqrt_guess(dve, link, ly[:, :], lx[:, :]))
            y = ly[:, :].bitcast(F32)
            for _ in range(3):
                link(dve.scalar_tensor_tensor(lt[:, :], y, -0.5, y, ALU.mult, ALU.mult))
                link(dve.tensor_tensor(lt[:, :], lt[:, :], lx[:, :], ALU.mult))
                link(dve.scalar_tensor_tensor(y, lt[:, :], 1.5, y, ALU.add, ALU.mult))
            dve.wait_ge(consts, 3)
            dve.tensor_tensor(diag[:, :, :], ident[:, :].unsqueeze(1).to_broadcast([P, TT, P]),
                              ly[:, :].bitcast(F32).unsqueeze(2).to_broadcast([P, TT, P]),
                              ALU.mult).then_inc(dg_rdy, 1)
            full = NG - 1
            rest = TOK - full * GTOK
            dve.wait_ge(ph_rdy, 1)
            dve.tensor_tensor(pl[:, 0:full, 0:GTOK], pt[:, 0:full * GTOK].rearrange("p (g q) -> p g q", q=GTOK),
                              ph[:, 0:full, 0:GTOK].bitcast(F32), ALU.subtract)
            dve.tensor_tensor(pl[:, full, 0:rest], pt[:, full * GTOK:], ph[:, full, 0:rest].bitcast(F32),
                              ALU.subtract).then_inc(pl_rdy, 1)
            dve.wait_ge(ld_lam, 16)
            link(dve.tensor_tensor(lamp[:, :, :], lamt[:, :, 0, :], lamt[:, :, 1, :], ALU.mult))
            dve.tensor_reduce(lams[:, :], lamp[:, :, :], AX.X, ALU.add).then_inc(lsum_rdy, 1)

            def m_lo(f):
                dve.wait_ge(mh_rdy, f + 1)
                dve.tensor_tensor(ml[:, f * PIECE:(f + 1) * PIECE], m_acc[f % 4][:, 0:PIECE],
                                  mh[:, f * PIECE:(f + 1) * PIECE].bitcast(F32), ALU.subtract).then_inc(ml_rdy, 1)

            for f in range(NPC - 1):
                m_lo(f)
                if f == 5:
                    dve.wait_ge(rb_rdy, 1)
                    dve.wait_ge(zeros, 1)
                    dve.wait_ge(consts, 6)
                    link(dve.tensor_tensor(rsel[:, :, :], r_b[:, :].rearrange("p (g q) -> p g q", q=GTOK),
                                           sel[:, :].unsqueeze(1).to_broadcast([P, NG, GTOK]), ALU.mult))
                    link(dve.tensor_reduce(rq[:, 0:NG], rsel[:, :, :], AX.X, ALU.add))
                    dve.tensor_scalar(rq8[:, :], rq[:, :], DH ** -0.5, None, ALU.mult)
                    pairs = rq[:, :].rearrange("p (t g) -> p t g", g=2)
                    for i in range(2):
                        last = dve.tensor_copy(rk[GP * i:GP * i + GP, :], pairs[GP * i:GP * i + GP, :, i])
                    last.then_inc(rk_rdy, 1)
            def evacuate(u0, u1):
                for u in range(u0, u1):
                    if is_q(u):
                        continue
                    kind, half, c = uses[u]
                    dve.wait_ge(ring_mm, u + 1)
                    if kind == "qk":
                        g0, g1 = groups(half)
                        t0, t1 = g0 * GTOK, g1 * GTOK
                        dve.scalar_tensor_tensor(kt[:, c - NPAIR, t0:t1], ring[u % 3][:, 0:t1 - t0], mt[:, c, P:FW],
                                                 r_b[:, t0:t1], ALU.add, ALU.mult).then_inc(kv_ev, 1)
                    else:
                        dve.tensor_tensor(v[:, half, :], ring[u % 3], cv_b[:, :], ALU.add).then_inc(kv_ev, 1)

            def threshold(k, total):
                dve.wait_ge(ab_mm, k + 1)
                link(dve.tensor_scalar(am[:, k:k + 1], total, 1.0 / (D * HID), 1e-5, ALU.mult, ALU.max))
                dve.tensor_scalar(thr[:, k:k + 1], am[:, k:k + 1], 0.7, None, ALU.mult).then_inc(thr_rdy, 1)
                dve.wait_ge(thr_rdy, k + 1)

            def ternary(q, w, k):
                return dve.scalar_tensor_tensor(q, w, thr[:, k:k + 1], q, ALU.is_gt, ALU.mult)

            def minus_max(g):
                s3 = s_acc[g % 2].rearrange("p (c k) -> p c k", k=GP)
                dve.wait_ge(s_mm, g + 1)
                link(dve.tensor_reduce(mx[:, g % 2, :], s3, AX.X, ALU.max))
                if g >= 3:
                    dve.wait_ge(a_rdy, g - 2)
                dve.tensor_tensor(e[g % 3][:, :, :], s3, mx[:, g % 2, :].unsqueeze(2).to_broadcast([P, NPAIR, GP]),
                                  ALU.subtract).then_inc(d_rdy, 1)

            def sums(g):
                dve.wait_ge(e_rdy, g + 1)
                link(dve.tensor_reduce(ssum[:, g % 2, :], e[g % 3][:, :, :], AX.X, ALU.add))
                link(dve.reciprocal(sinv[:, g, :], ssum[:, g % 2, :]))
                dve.scalar_tensor_tensor(ratio[:, g % 3, :], ssum[:, g % 2, 0:NHP], neglam[:, :],
                                         sinv[:, g, NHP:], ALU.mult, ALU.mult).then_inc(rat_rdy, 1)

            def sum_squares(T):
                n_gp = len(gps(T))
                dve.wait_ge(on_rdy, T + 1)
                dve.tensor_reduce(ms[:, 2 * T:2 * T + n_gp].rearrange("p g j c -> p (g j c)"),
                                  osq[T % 2][:, 0:n_gp].rearrange("p g j (c d) -> p (g j c) d", d=RMSW),
                                  AX.X, ALU.add).then_inc(ms_rdy, 1)

            def mean_squares(b):
                g0, m = batch_groups(b)[0], len(batch_groups(b))
                si = sinv[:, g0:g0 + m, 0:NHP]
                link(dve.scalar_tensor_tensor(sinv2[:, 0:m, :], si, 1.0 / RMSW / (1 - L_INIT) ** 2, si,
                                              ALU.mult, ALU.mult))
                dve.wait_ge(ms_rdy, BATCHES[b][1])
                s2 = sinv2[:, 0:m, :].rearrange("p g j -> p (g j)").unsqueeze(2).to_broadcast([P, NHP * m, RMSW])
                link(dve.tensor_tensor(nx[:, b, 0:m].rearrange("p g j c -> p (g j) c"),
                                       ms[:, g0:g0 + m].rearrange("p g j c -> p (g j) c"), s2, ALU.mult))
                dve.tensor_scalar(nx[:, b, 0:m], nx[:, b, 0:m], RMS_EPS / (1 - L_INIT) ** 2, None,
                                  ALU.add).then_inc(msq_rdy, 1)

            def rms_factors(b):
                g0, m = batch_groups(b)[0], len(batch_groups(b))
                dve.wait_ge(root_rdy, b + 1)
                f = ny[:, b, 0:m]
                link(dve.reciprocal(f, nt[:, b, 0:m]))
                dve.tensor_tensor(f, f, sinv[:, g0:g0 + m, 0:NHP].unsqueeze(3).to_broadcast([P, m, NHP, RMSW]),
                                  ALU.mult).then_inc(rms_rdy, 1)

            def wo_lo(k):
                dve.wait_ge(woh_rdy, k + 1)
                dve.tensor_tensor(wo_l[:, k, :], wo_s[:, k, :], wo_h[k][:, :].bitcast(F32),
                                  ALU.subtract).then_inc(wol_dve_rdy, 1)

            def o_lo(T):
                dve.wait_ge(ot_rdy, T + 1)
                for i in gps(T):
                    g = 2 * T + i
                    for j in range(2):
                        w = slice(g * GTOK, (g + 1) * GTOK)
                        last = dve.tensor_tensor(
                            otl[:, 2 * j:2 * j + 2, w],
                            ot_acc[T % 2][:, (2 * i + j) * P:(2 * i + j + 1) * P].rearrange(
                                "p (h q) -> p h q", q=GP)[:, :, 0:GTOK],
                            ot[:, 2 * j:2 * j + 2, w].bitcast(F32), ALU.subtract)
                last.then_inc(otl_rdy, 1)

            def z_lo(i):
                dve.wait_ge(zth_rdy, i + 1)
                dve.tensor_tensor(ztl[:, :, i * P:(i + 1) * P], zt_acc[i % 2].rearrange("p (k t) -> p k t", t=P),
                                  zth[:, :, i * P:(i + 1) * P], ALU.subtract).then_inc(ztl_rdy, 1)

            def residual(i):
                dve.wait_ge(wo_mm, i + 1)
                dve.tensor_tensor(h[:, i, :], h[:, i, :], wo_acc[i % 2], ALU.add).then_inc(h1_rdy, 1)
                dve.wait_ge(h1_rdy, i + 1)
                link(dve.bn_stats(bnst[:, i, :], h[:, i, :]))
                link(dve.bn_aggr(stat2[:, i, :], bnst[:, i, :]))

            def z_vars(n):
                t0, t1 = LN_TILES[n]
                dve.tensor_scalar(lx[:, t0:t1], stat2[:, t0:t1, 1], LN_EPS, Z_SCALE ** -2,
                                  ALU.add, ALU.mult).then_inc(var_rdy, 1)

            def z_factors(n):
                t0, t1 = LN_TILES[n]
                dve.wait_ge(lroot_rdy, n + 1)
                link(dve.reciprocal(linv[:, t0:t1], lt[:, t0:t1]))
                dve.scalar_tensor_tensor(lshift[:, t0:t1], stat2[:, t0:t1, 0], -1.0, linv[:, t0:t1],
                                         ALU.mult, ALU.mult).then_inc(shift_rdy, 1)

            def ternary_fc(k):
                ternary(qfc[:, k, :], fc_raw[:, k, :], 0).then_inc(qfc_rdy, 1)

            def ternary_proj(c):
                ternary(qproj[:, c, :], proj_raw[:, c, :], 1).then_inc(qproj_rdy, 1)

            dve.wait_ge(mt_rdy, NPC)
            evacuate(0, 2)
            m_lo(NPC - 1)
            evacuate(2, 8)
            dve.tensor_tensor(diag[:, 0:KD, :], ident[:, :].unsqueeze(1).to_broadcast([P, KD, P]),
                              mt[:, 2 * NPAIR:, P].unsqueeze(2).to_broadcast([P, KD, P]), ALU.mult).then_inc(dv_rdy, 1)
            evacuate(8, 14)
            dve.wait_ge(cv_mm, 1)
            dve.tensor_copy(cv_b[:, :], cv_acc).then_inc(cv_rdy, 1)
            dve.wait_ge(cv_rdy, 1)
            evacuate(14, n_first)
            dve.wait_ge(lexp_rdy, 1)
            link(dve.scalar_tensor_tensor(neglam[:, :], lame[:, 1:2], L_INIT, lame[:, 0:1], ALU.subtract, ALU.subtract))
            for g in range(NG):
                if g == NG - 1:
                    sums(g - 1)
                minus_max(g)
                evacuate(fill[g], fill[g + 1])
                if 1 <= g < NG - 1:
                    sums(g - 1)
                if g >= 6 and g % 2 == 0:
                    sum_squares((g - 6) // 2)
                if g == 9:
                    dve.wait_ge(abs_rdy, KD)
                    dve.tensor_reduce(psm[:, 0:1], part[:, 0, 0:KD], AX.X, ALU.add).then_inc(ab_rdy, 1)
            mean_squares(0)
            sums(NG - 1)
            threshold(0, abs_acc[0])
            wo_lo(1)
            wo_lo(2)
            rms_factors(0)
            sum_squares(3)
            sum_squares(4)
            wo_lo(3)
            sum_squares(5)
            mean_squares(1)
            o_lo(0)
            o_lo(1)
            rms_factors(1)
            o_lo(2)
            ternary_fc(0)
            ternary_fc(1)
            o_lo(3)
            residual(0)
            o_lo(4)
            residual(1)
            z_vars(0)
            o_lo(5)
            z_factors(0)
            residual(2)
            z_vars(1)
            z_factors(1)
            z_lo(0)
            z_lo(1)
            z_lo(2)
            residual(3)
            residual(4)
            z_vars(2)

            def g_lo(k):
                half, c = divmod(k, HC)
                t0, t1 = FFN_TILES[half]
                dve.wait_ge(gh_rdy, k + 1)
                dve.tensor_tensor(gl[:, c, t0 * P:t1 * P], squ[k % 2][:, 0:(t1 - t0) * P], gh[:, c, t0 * P:t1 * P],
                                  ALU.subtract).then_inc(gl_rdy, 1)

            for k in range(2 * HC):
                g_lo(k)
                if k == 0:
                    z_factors(2)
                    dve.wait_ge(abs_rdy, KD + HC)
                    dve.tensor_reduce(psm[:, 1:2], part[:, 1, :], AX.X, ALU.add).then_inc(ab_rdy, 1)
                if k == 2:
                    threshold(1, abs_acc[1])
                if 3 <= k < 3 + HC:
                    ternary_proj(k - 3)
                if k in (4, 6):
                    z_lo(k // 2 + 1)
            link(dve.tensor_scalar(sout[:, :], am[:, 0:1], am[:, 0:1], am[:, 1:2], ALU.mult, ALU.mult))
            link(dve.tensor_scalar(sout[:, :], sout[:, :], H_SCALE ** -2, None, ALU.mult))
            for m, (i, d0, d1) in enumerate(OUT_PIECES):
                dve.wait_ge(pj_mm, m + 1)
                if m >= 2:
                    dve.wait_ge(st_out[m % 2], 16 * (m // 2))
                dve.scalar_tensor_tensor(orow[m % 2][:, 0:d1 - d0], pj_acc[m % 2][:, 0:d1 - d0], sout[:, :],
                                         h[:, i, d0:d1], ALU.mult, ALU.add).then_inc(o_rdy, 1)

        @block.tensor
        def _(pe):
            def mm(o, l, r, start, stop):
                return pe.matmul(o, l, r, start=start, stop=stop, skip_group_check=True)

            pe.wait_ge(consts, 1)
            pe.wait_ge(ld_wpos, 16)
            for k in range(KD):
                last = mm(mean_acc[:, 0:FW], mean_w[:, :], wpos[:, k, :], k == 0, k == KD - 1)
            last.then_inc(mean_rdy, 1)
            pe.wait_ge(ld_x, 16)
            pe.wait_ge(ld_wcol, 16)
            for i in range(TT):
                mm(h_acc[i], pt[:, i * P:(i + 1) * P], wcol[:, :], True, True).then_inc(h_mm, 1)

            def transpose_piece(f):
                pe.wait_ge(mt_rdy, f + 1)
                if f >= 4:
                    pe.wait_ge(ml_rdy, f - 3)
                elif f == 0:
                    pe.wait_ge(h_ev, TT)
                for c in range(2):
                    last = pe.transpose(m_acc[f % 4][:, c * P:(c + 1) * P], mt[:, 2 * f + c, 0:P], ident[:, :])
                last.then_inc(tr_mm, 1)

            pe.wait_ge(wc_rdy, 1)
            pe.wait_ge(consts, 3)
            for f in range(NPC):
                pe.wait_ge(ld_qkv[f], 16)
                if f >= 2:
                    pe.wait_ge(mt_rdy, f - 1)
                for c in range(2):
                    for k in range(KD):
                        last = mm(fold_acc[f % 2][:, c * FWS:c * FWS + FW], wqkv_s[:, f, k, c * P:(c + 1) * P],
                                  wc[:, k, :], k == 0, k == KD - 1)
                last.then_inc(fold_mm, 1)
                if f >= 1:
                    transpose_piece(f - 1)
                if f == 4:
                    pe.wait_ge(dg_rdy, 1)
                    dg = diag[:, :, :].rearrange("p t q -> p (t q)")
                    for i in range(2):
                        last = mm(rb_acc[i][:, 0:320], ones[:, :], dg[:, 320 * i:320 * i + 320], True, True)
                    last.then_inc(rb_mm, 1)

            def project(u0, u1):
                for u in range(u0, u1):
                    kind, half, c = uses[u]
                    if u >= 3:
                        pe.wait_ge(*evacuated(u - 3))
                    if u < n_first:
                        pe.wait_ge(ml_rdy, c // 2 + 1 if kind == "qk" else NPC)
                    if kind == "qk":
                        g0, g1 = groups(half)
                        o = ring[u % 3][:, 0:(g1 - g0) * GTOK]
                        w = slice(c * P, (c + 1) * P)
                        mm(o, mh[:, w], ph[:, g0:g1, 0:GTOK], True, False)
                        mm(o, mh[:, w], pl[:, g0:g1, 0:GTOK], False, False)
                        last = mm(o, ml[:, w], ph[:, g0:g1, 0:GTOK], False, True)
                    else:
                        T = half
                        o = ring[u % 3]
                        xh = ph[:, 2 * T:2 * T + 2, :].rearrange("p g q -> p (g q)")
                        xl = pl[:, 2 * T:2 * T + 2, :].rearrange("p g q -> p (g q)")
                        mm(o, xh, mh[:, 4 * D:], True, False)
                        mm(o, xh, ml[:, 4 * D:], False, False)
                        last = mm(o, xl, mh[:, 4 * D:], False, True)
                    last.then_inc(ring_mm, 1)

            pe.wait_ge(zeros, 1)
            pe.wait_ge(pl_rdy, 1)
            pe.wait_ge(rb_rdy, 1)
            pe.wait_ge(ml_rdy, NPC - 2)
            project(0, 1)
            transpose_piece(NPC - 1)
            project(1, 12)
            pe.wait_ge(dv_rdy, 1)
            mm(cv_acc, ones[:, :], diag[:, 0:KD, :].rearrange("p t q -> p (t q)"), True, True).then_inc(cv_mm, 1)
            project(12, n_first)
            pe.wait_ge(consts, 7)
            pe.wait_ge(cv_rdy, 1)

            def scores(g):
                if g in (0, HALF_G[0]):
                    u = (2 * NPAIR if g == 0 else n_second) - 1
                    nq = sum(is_q(w) for w in range(u + 1))
                    pe.wait_ge(q_ev, nq)
                    pe.wait_ge(kv_ev, u + 1 - nq)
                if g >= 2:
                    pe.wait_ge(d_rdy, g - 1)
                mm(s_acc[g % 2], ident_b[:, :], mask[:, :, :].rearrange("p c k -> p (c k)"), True, False)
                t = slice(g * GTOK, (g + 1) * GTOK)
                for c in range(NPAIR):
                    for r0 in (0, GP):
                        last = mm(s_acc[g % 2][r0:r0 + GTOK, c * GP:c * GP + GTOK], qt[r0:r0 + GP, c, t],
                                  kt[r0:r0 + GP, c, t], False, c == NPAIR - 1)
                last.then_inc(s_mm, 1)

            def transpose_a(T):
                pe.wait_ge(a_rdy, min(2 * T + 2, NG))
                if T >= 1:
                    pe.wait_ge(at_rdy, T)
                for j in range(NHP):
                    last = pe.transpose(at_acc[T][:, j * P:(j + 1) * P],
                                        a[T % 2][:, j, :, :].rearrange("p g k -> p (g k)"), ident[:, :])
                last.then_inc(at_mm, 1)

            def apply(T):
                pe.wait_ge(at_rdy, T + 1)
                pe.wait_ge(*evacuated(n_second + T - 3 if T >= 3 else 2 * NPAIR + T))
                if T >= 1:
                    pe.wait_ge(on_rdy, T)
                for i in gps(T):
                    r0 = GP * i
                    for j in range(NHP):
                        for s in range(2):
                            last = mm(o_ps[GP * s:GP * s + GP, i, j * DH:(j + 1) * DH],
                                      ats[T % 2][r0:r0 + GTOK, j, s, :],
                                      v[r0:r0 + GTOK, T, (2 * j + s) * DH:(2 * j + s + 1) * DH], True, True)
                last.then_inc(av_mm, 1)

            def transpose_o(T):
                pe.wait_ge(on2_rdy, T + 1)
                if T >= 2:
                    pe.wait_ge(otl_rdy, T - 1)
                for i in gps(T):
                    for j in range(2):
                        last = pe.transpose(ot_acc[T % 2][:, (2 * i + j) * P:(2 * i + j + 1) * P],
                                            on[:, T, i, 2 * j:2 * j + 2, :].rearrange("p j d -> p (j d)"), ident[:, :])
                last.then_inc(ot_mm, 1)

            def keep_busy(n):
                for _ in range(n):
                    mm(wo_acc[0][:, 0:P], ones[:, :], mean_w[:, :], True, True)

            def transpose_z(i):
                pe.wait_ge(z_rdy, i + 1)
                if i == 1:
                    pe.wait_ge(otl_rdy, NT)
                if i >= 2:
                    pe.wait_ge(ztl_rdy, i - 1)
                for k in range(KD):
                    last = pe.transpose(zt_acc[i % 2][:, k * P:(k + 1) * P], z[i % 3][:, k * P:(k + 1) * P], ident[:, :])
                last.then_inc(zt_mm, 1)

            def project_out(i):
                t = slice(i * P, (i + 1) * P)
                pe.wait_ge(otl_rdy, min(NT, -(-(i + 1) * P // (2 * GTOK))))
                if i >= 2:
                    pe.wait_ge(h1_rdy, i - 1)
                for k in range(KD):
                    mm(wo_acc[i % 2], ot[:, k, t], wo_h[k][:, :], k == 0, False)
                    mm(wo_acc[i % 2], ot[:, k, t], wo_l[:, k, :], False, False)
                    last = mm(wo_acc[i % 2], otl[:, k, t], wo_h[k][:, :], False, k == KD - 1)
                last.then_inc(wo_mm, 1)

            for g in range(NG):
                scores(g)
                project(fill[g], fill[g + 1])
                if g >= 4 and g % 2 == 0:
                    transpose_a((g - 4) // 2)
                if g >= 5 and g % 2 == 1:
                    if g == 9:
                        pe.wait_ge(*evacuated(n_uses - 1))
                        keep_busy(4)
                    apply((g - 5) // 2)
            keep_busy(4)
            apply(3)
            pe.wait_ge(ab_rdy, 1)
            mm(abs_acc[0], ones[:, :], psm[:, 0:1], True, True).then_inc(ab_mm, 1)
            transpose_a(4)
            keep_busy(6)
            apply(4)
            transpose_a(5)
            keep_busy(4)
            apply(5)
            keep_busy(2)
            pe.wait_ge(thr_rdy, 1)
            transpose_o(0)
            transpose_o(1)
            keep_busy(2)
            pe.wait_ge(wol_rdy, 1)
            pe.wait_ge(wol_dve_rdy, 3)
            transpose_o(2)
            project_out(0)
            transpose_o(3)
            project_out(1)
            transpose_o(4)
            transpose_o(5)
            project_out(2)
            project_out(3)
            transpose_z(0)
            transpose_z(1)
            project_out(4)
            transpose_z(2)

            pe.wait_ge(qfc_rdy, 2)
            pe.wait_ge(qfc_pool_rdy, KD - 2)
            for half in range(2):
                t0, t1 = FFN_TILES[half]
                pe.wait_ge(ztl_rdy, t1 - 1 if half == 0 else t1)
                for c in range(HC):
                    u = half * HC + c
                    if u >= 2:
                        pe.wait_ge(rel_rdy, u - 1)
                    for a0, a1 in ((t0, t1 - 1), (t1 - 1, t1)) if u == 0 else ((t0, t1),):
                        t = slice(a0 * P, a1 * P)
                        if u == 0:
                            pe.wait_ge(ztl_rdy, a1)
                        for k in range(KD):
                            w = qfc[:, k, c * P:(c + 1) * P]
                            o = fc_acc[u % 2][:, (a0 - t0) * P:(a1 - t0) * P]
                            mm(o, w, zth[:, k, t], k == 0, False)
                            last = mm(o, w, ztl[:, k, t], False, k == KD - 1)
                    last.then_inc(fc_mm, 1)
                    if u == 3:
                        pe.wait_ge(ab_rdy, 2)
                        mm(abs_acc[1], ones[:, :], psm[:, 1:2], True, True).then_inc(ab_mm, 1)
                    if half == 0 and c in (4, 6):
                        transpose_z(c // 2 + 1)
            pe.wait_ge(qproj_rdy, HC)
            pe.wait_ge(thr_rdy, 2)
            for n, (i, d0, d1) in enumerate(OUT_PIECES):
                t = slice(i * P, (i + 1) * P)
                pe.wait_ge(gl_rdy, HC if i < FFN_TILES[0][1] else 2 * HC)
                if n >= 2:
                    pe.wait_ge(o_rdy, n - 1)
                for c in range(HC):
                    mm(pj_acc[n % 2][:, 0:d1 - d0], gh[:, c, t], qproj[:, c, d0:d1], c == 0, False)
                    last = mm(pj_acc[n % 2][:, 0:d1 - d0], gl[:, c, t], qproj[:, c, d0:d1], False, c == HC - 1)
                last.then_inc(pj_mm, 1)


def kernel(x, L0_tok_W, L0_tok_b, L0_attn_l_q1, L0_attn_l_k1, L0_attn_l_q2, L0_attn_l_k2, L0_attn_wq, L0_attn_wk,
           L0_attn_wv, L0_attn_wo, L0_ffn_w_fc, L0_ffn_w_proj):
    import concourse.bacc as bacc
    import numpy as np
    from concourse.bass_utils import run_bass_kernel_spmd

    f = np.ascontiguousarray
    xs = np.asarray(x)[:, :, 0]
    patches = np.stack([xs[:, STRIDE * n:STRIDE * n + P] for n in range(NPATCH)], axis=1)
    W, bias = np.asarray(L0_tok_W), np.asarray(L0_tok_b)
    wb = np.concatenate([W, bias[:, None]], axis=1)
    wqkv = np.concatenate([np.asarray(L0_attn_wq), np.asarray(L0_attn_wk), np.asarray(L0_attn_wv)])
    wo = np.asarray(L0_attn_wo)
    arrays = {
        "xT": f(patches.reshape(TOK, P).T),
        "w_pos": f(wb.reshape(KD, P, FW).transpose(1, 0, 2)),
        "w_col": f(W.T),
        "b": f(bias),
        "lam": f(np.stack([np.asarray(t) for t in (L0_attn_l_q1, L0_attn_l_k1, L0_attn_l_q2, L0_attn_l_k2)])
                 .reshape(2, 2, NH)),
        "wqkv": f(wqkv.reshape(NPC, PIECE, KD, P).transpose(0, 3, 2, 1)),
        "wo": f(wo.T.reshape(2, 2, 2, DH, D).transpose(1, 3, 0, 2, 4).reshape(P, KD, D)),
        "w_fc": f(np.asarray(L0_ffn_w_fc).reshape(HID, KD, P).transpose(2, 1, 0)),
        "w_proj": f(np.asarray(L0_ffn_w_proj).reshape(D, HC, P).transpose(2, 1, 0)),
    }
    nc = bacc.Bacc("TRN2", target_bir_lowering=False, num_devices=1)
    args = [nc.dram_tensor(n, t.shape, F32, kind="ExternalInput").ap() for n, t in arrays.items()]
    out = nc.dram_tensor("out", (TT, P, D), F32, kind="ExternalOutput").ap()
    audio_block(nc, *args, out)
    r = run_bass_kernel_spmd(nc, [arrays], core_ids=[0])
    return r.results[0]["out"].reshape(NB, NPATCH, D)
```
